# Optimizing a Trainium2 kernel written in Bass

```python
import numpy as np
import jax
import jax.numpy as jnp

def _softmax(x, axis=-1):
    return jax.nn.softmax(x, axis=axis)

def _gelu(x):
    return jax.nn.gelu(x, approximate=True)

def _silu(x):
    return jax.nn.silu(x)

def _sigmoid(x):
    return jax.nn.sigmoid(x)

def _layernorm(x, axis=-1, eps=1e-05):
    m = jnp.mean(x, axis=axis, keepdims=True)
    v = jnp.var(x, axis=axis, keepdims=True)
    return (x - m) / jnp.sqrt(v + eps)

def _scatter_add(tgt, idx, src, axis=0):
    return tgt.at[idx].add(src)

def _segment_sum(src, seg, n):
    return jax.ops.segment_sum(src, seg, n)
kernel_name = 'mk_seq_preln_d1_jaxref_r4_ac9fea'

def setup_inputs(seed: int=0):
    np.random.seed(seed)
    _w = jnp.asarray

    def _L0_attn_setup():
        import jax, jax.numpy as jnp
        import numpy as np
        MODEL_DIM = 256
        NUM_HEADS = 16
        HEAD_DIM = MODEL_DIM // NUM_HEADS
        WINDOW_SIZE = 64
        BATCH = 1
        SEQ_LEN = 1024

        def local_causal_bias(seq_len, window_size, dtype):
            i = jnp.arange(seq_len)[:, None]
            j = jnp.arange(seq_len)[None, :]
            allowed = (j <= i) & (j > i - window_size)
            neg_inf = jnp.array(-jnp.inf, dtype=dtype)
            return jnp.where(allowed, jnp.array(0.0, dtype=dtype), neg_inf)
        key = jax.random.key(seed)
        k_h, k_q, k_k, k_v, k_o = jax.random.split(key, 5)
        s = 1.0 / np.sqrt(MODEL_DIM)
        hidden = jax.random.normal(k_h, (BATCH, SEQ_LEN, MODEL_DIM), dtype=jnp.float32)
        Wq = jax.random.normal(k_q, (MODEL_DIM, MODEL_DIM), dtype=jnp.float32) * s
        Wk = jax.random.normal(k_k, (MODEL_DIM, MODEL_DIM), dtype=jnp.float32) * s
        Wv = jax.random.normal(k_v, (MODEL_DIM, MODEL_DIM), dtype=jnp.float32) * s
        Wo = jax.random.normal(k_o, (MODEL_DIM, MODEL_DIM), dtype=jnp.float32) * s
        return {'hidden': hidden, 'Wq': Wq, 'Wk': Wk, 'Wv': Wv, 'Wo': Wo}
    _L0_attn_in = _L0_attn_setup()

    def _L0_ffn_setup():
        import jax, jax.numpy as jnp
        import numpy as np
        H = 256
        I = 128
        E = 8
        K = 2
        SI = I * 2
        B, S = (2, 256)

        def _mlp(x, gw, uw, dw):
            return jax.nn.silu(x @ gw.T) * (x @ uw.T) @ dw.T
        key = jax.random.key(seed)
        ks = jax.random.split(key, 9)
        s = 0.02
        return {'x': jax.random.normal(ks[0], (B, S, H), jnp.float32), 'gate_w': jax.random.normal(ks[1], (E, H), jnp.float32) * s, 'lb_bias': jnp.zeros((E,), jnp.float32), 'expert_gate_w': jax.random.normal(ks[2], (E, I, H), jnp.float32) * s, 'expert_up_w': jax.random.normal(ks[3], (E, I, H), jnp.float32) * s, 'expert_down_w': jax.random.normal(ks[4], (E, H, I), jnp.float32) * s, 'shared_gate_w': jax.random.normal(ks[5], (SI, H), jnp.float32) * s, 'shared_up_w': jax.random.normal(ks[6], (SI, H), jnp.float32) * s, 'shared_down_w': jax.random.normal(ks[7], (H, SI), jnp.float32) * s}
    _L0_ffn_in = _L0_ffn_setup()
    _d = {'L0_attn_hidden': _L0_attn_in['hidden'], 'L0_attn_Wq': _L0_attn_in['Wq'], 'L0_attn_Wk': _L0_attn_in['Wk'], 'L0_attn_Wv': _L0_attn_in['Wv'], 'L0_attn_Wo': _L0_attn_in['Wo'], 'L0_ffn_gate_w': _L0_ffn_in['gate_w'], 'L0_ffn_lb_bias': _L0_ffn_in['lb_bias'], 'L0_ffn_expert_gate_w': _L0_ffn_in['expert_gate_w'], 'L0_ffn_expert_up_w': _L0_ffn_in['expert_up_w'], 'L0_ffn_expert_down_w': _L0_ffn_in['expert_down_w'], 'L0_ffn_shared_gate_w': _L0_ffn_in['shared_gate_w'], 'L0_ffn_shared_up_w': _L0_ffn_in['shared_up_w'], 'L0_ffn_shared_down_w': _L0_ffn_in['shared_down_w']}
    _x0 = _d['L0_attn_hidden']
    _d['L0_attn_hidden'] = jax.random.normal(jax.random.fold_in(jax.random.key(seed), 1), (4, 1024, 256), dtype=_x0.dtype)
    del _x0
    return _d

def reference(L0_attn_hidden, L0_attn_Wq, L0_attn_Wk, L0_attn_Wv, L0_attn_Wo, L0_ffn_gate_w, L0_ffn_lb_bias, L0_ffn_expert_gate_w, L0_ffn_expert_up_w, L0_ffn_expert_down_w, L0_ffn_shared_gate_w, L0_ffn_shared_up_w, L0_ffn_shared_down_w):

    def _L0_attn_ref(hidden, Wq, Wk, Wv, Wo):
        import jax, jax.numpy as jnp
        import numpy as np
        MODEL_DIM = 256
        NUM_HEADS = 16
        HEAD_DIM = MODEL_DIM // NUM_HEADS
        WINDOW_SIZE = 64
        BATCH = 1
        SEQ_LEN = 1024

        def local_causal_bias(seq_len, window_size, dtype):
            i = jnp.arange(seq_len)[:, None]
            j = jnp.arange(seq_len)[None, :]
            allowed = (j <= i) & (j > i - window_size)
            neg_inf = jnp.array(-jnp.inf, dtype=dtype)
            return jnp.where(allowed, jnp.array(0.0, dtype=dtype), neg_inf)
        B, S, D = hidden.shape

        def proj(x, W):
            y = jnp.einsum('bsd,ed->bse', x, W)
            return y.reshape(B, S, NUM_HEADS, HEAD_DIM).transpose(0, 2, 1, 3)
        q = proj(hidden, Wq)
        k = proj(hidden, Wk)
        v = proj(hidden, Wv)
        scale = 1.0 / np.sqrt(HEAD_DIM)
        bias = local_causal_bias(S, WINDOW_SIZE, hidden.dtype)
        scores = jnp.einsum('bhqd,bhkd->bhqk', q, k) * scale + bias
        attn = jax.nn.softmax(scores, axis=-1)
        out = jnp.einsum('bhqk,bhkd->bhqd', attn, v)
        out = out.transpose(0, 2, 1, 3).reshape(B, S, D)
        return jnp.einsum('bsd,ed->bse', out, Wo)

    def _L0_ffn_ref(x, gate_w, lb_bias, expert_gate_w, expert_up_w, expert_down_w, shared_gate_w, shared_up_w, shared_down_w):
        import jax, jax.numpy as jnp
        import numpy as np
        H = 256
        I = 128
        E = 8
        K = 2
        SI = I * 2
        B, S = (2, 256)

        def _mlp(x, gw, uw, dw):
            return jax.nn.silu(x @ gw.T) * (x @ uw.T) @ dw.T
        b, s, h = x.shape
        xf = x.reshape(-1, h)
        logits = xf @ gate_w.T + lb_bias
        scores = jax.nn.sigmoid(logits.astype(jnp.float32))
        topw, topi = jax.lax.top_k(scores, K)
        topw = (topw / (topw.sum(-1, keepdims=True) + 1e-08)).astype(x.dtype)
        out = jnp.zeros_like(xf)
        for e in range(E):
            m = topi == e
            sel = m.any(axis=-1)
            cnt = m.sum()
            wmean = (topw * m).sum() / jnp.maximum(cnt, 1).astype(topw.dtype)
            y = _mlp(xf, expert_gate_w[e], expert_up_w[e], expert_down_w[e])
            out = out + jnp.where(sel[:, None], y * wmean, jnp.zeros((), x.dtype))
        out = out.reshape(b, s, h)
        out = out + _mlp(x, shared_gate_w, shared_up_w, shared_down_w)
        return out
    x = L0_attn_hidden
    x = x + _L0_attn_ref(_layernorm(x, axis=-1), L0_attn_Wq, L0_attn_Wk, L0_attn_Wv, L0_attn_Wo)
    x = x + _L0_ffn_ref(_layernorm(x, axis=-1), L0_ffn_gate_w, L0_ffn_lb_bias, L0_ffn_expert_gate_w, L0_ffn_expert_up_w, L0_ffn_expert_down_w, L0_ffn_shared_gate_w, L0_ffn_shared_up_w, L0_ffn_shared_down_w)
    return x

_drawn_inputs = setup_inputs


def setup_inputs(seed=0):
    import zlib

    import numpy as np

    out = dict(_drawn_inputs(seed))
    spreads = {'L0_ffn_lb_bias': (0.0, 0.8)}
    factors = {'L0_ffn_gate_w': 8.0,
     'L0_ffn_expert_gate_w': 6.958,
     'L0_ffn_expert_up_w': 6.864,
     'L0_ffn_expert_down_w': 6.879,
     'L0_ffn_shared_gate_w': 3.461,
     'L0_ffn_shared_up_w': 3.425,
     'L0_ffn_shared_down_w': 3.429}
    for name, (base, spread) in spreads.items():
        noise = np.random.default_rng([zlib.crc32(name.encode()), seed]).standard_normal(out[name].shape)
        drawn = base * np.exp(spread * noise) if base else spread * noise
        out[name] = jnp.asarray(drawn.astype(out[name].dtype))
    for name, factor in factors.items():
        out[name] = (out[name] * factor).astype(out[name].dtype)
    return out
```

```python
from contextlib import ExitStack

import concourse.bass as bass
from concourse import mybir

F32 = mybir.dt.float32
F32R = mybir.dt.float32r
BF16 = mybir.dt.bfloat16
ALU = mybir.AluOpType
ACT = mybir.ActivationFunctionType
AX = mybir.AxisListType

P = 128
D = 256
KT = D // P
H, HD = 16, 16
WIN = 64
GT = 256
TPG = GT // P
BPG = GT // WIN
HPT = P // HD
VC = HD + 1
E = 8
EI = 128
MASKED = -1.0e30
EPS = 1e-5


def layer(nc, x, wqkvo, wgate, bias, wffn, identity, out):
    T = x.shape[0]
    NT = T // P
    NG = T // GT
    GPB = 1024 // GT
    XC = 8
    NE = wffn.shape[1]

    with ExitStack() as ctx:
        def sb(name, shape, dt=F32):
            return ctx.enter_context(nc.sbuf_tensor(name, shape, dt))

        def sem(name):
            return ctx.enter_context(nc.semaphore(name))

        xs = sb("xs", [P, NT, D])
        y = sb("y", [P, TPG, D])
        qy = sb("qy", [P, 2, 2, KT, GT], F32R)
        qT, yT = qy[:, 0, :, :, :], qy[:, 1, :, :, :]
        wA = sb("wA", [P, 2, 4, KT, D], F32R)
        bd = sb("bd", [P, 2, 2 * KT * BPG, HPT * WIN], F32R)
        kT = sb("kT", [P, 2, 2, KT, BPG + 1, WIN], F32R)
        vt = sb("vt", [P, 2, TPG, H, VC])
        vm = sb("vm", [P, 2, TPG, H, VC])
        probs = sb("probs", [P, 2, KT * HPT * WIN])
        wraw = probs[:, :, :].rearrange("p a c -> p (a c)")
        mrow = sb("mrow", [2, 2, KT * HPT * WIN], F32R)
        rmax = sb("rmax", [P, 2, 32])
        negm = sb("negm", [32, 2, 32])
        negs = sb("negs", [32, 2, 2, 32], F32R)
        rden = sb("rden", [P, HPT])
        o = sb("o", [P, 2, BPG, P])
        oT = sb("oT", [P, 2, 2, BPG, WIN], F32R)
        z = sb("z", [P, TPG, D])
        zT = sb("zT", [P, 2, KT, GT], F32R)
        graw = sb("graw", [P, KT, E])
        wG = sb("wG", [P, 2, KT, 2, E], F32R)
        stats = sb("stats", [P, 2, TPG, 6])
        mv = sb("mv", [P, 2, TPG, 2])
        rstd = sb("rstd", [P, 2, TPG])
        mhalf, epsb = sb("mhalf", [P, TPG]), sb("epsb", [P, TPG])
        identf = sb("identf", [P, P])
        identb = sb("identb", [P, P], BF16)
        window_mask = sb("window_mask", [P, WIN], BF16)
        mask_first = sb("mask_first", [P, NG, WIN], BF16)
        maskf = sb("maskf", [P, 2, WIN])
        onesf = sb("onesf", [P, P])
        ones2 = sb("ones2", [2, P], F32R)
        logits = sb("logits", [P, NT, E])
        biasb = sb("biasb", [P, E])
        wfraw = sb("wfraw", [P, NE, 6 * P])

        bdflat = bd[:, :, :, :].rearrange("p a b c -> p (a b c)")
        wF = [bdflat[:, h * 8192:h * 8192 + NE * 6 * P].rearrange("p (e c) -> p e c", e=NE) for h in range(2)]

        ps = ctx.enter_context(nc.psum_tensor("ps", [P, 8, 512], F32))
        S = [ps[:, 2 * i:2 * i + 2, :] for i in range(2)]
        sg, hf = y, z
        hh = oT[:, :, :, :, :].rearrange("p a b c q -> p (a b c q)").rearrange("p (e a c) -> p e a c", e=2, a=2)
        esc = probs[:, 0, 0:NT * E].rearrange("p (t e) -> p t e", e=E)
        cmp = probs[:, 0, 256:256 + NT * E].rearrange("p (t e) -> p t e", e=E)
        rank = probs[:, 0, 512:512 + NT * E].rearrange("p (t e) -> p t e", e=E)

        wsel = probs[:, 1, 0:NT * NE].rearrange("p (t e) -> p t e", e=NE)
        lt = probs[:, 1, 512:512 + E * E].rearrange("p (e f) -> p e f", e=E)
        wsum, wmean = probs[:, 1, 640:640 + 2 * E], probs[:, 1, 672:672 + E]

        def zt_of(g, a, k):
            if isinstance(g, int):
                return qy[:, g % 2, a, k, :]
            return qy[:, bass.ds(g % 2, 1), a, k, :].rearrange("p o c -> p (o c)")

        PV, RT, BANK_A, BANK_B = 4, 5, 6, 7
        pv = ps[:, PV, 0:HPT * 2 * VC].rearrange("p (a b) -> p a b", a=HPT)

        s_x = [sem(f"x_loaded_{i}") for i in range(XC)]
        s_w = sem("weights_loaded")
        s_const = sem("constants_loaded")
        s_wf = sem("ffn_weights_loaded")
        s_pool = sem("pool_setup")
        s_setup = sem("constants_ready")
        s_wA = sem("attention_weights_split")
        s_wAl = sem("attention_weights_lo")
        s_bd0 = sem("bd_zeroed")
        s_bn = [sem(f"bn_stats_{i}_ready") for i in range(2)]
        s_st = [sem(f"mean_var_{i}_ready") for i in range(2)]
        s_ve = [sem(f"var_eps_{i}_ready") for i in range(2)]
        s_rs = [sem(f"rstd_{i}_ready") for i in range(2)]
        s_yz = [sem("y_ready"), sem("z_ready")]
        s_yTp, s_yTh, s_yTl = sem("yT_in_psum"), sem("yT_hi"), sem("yT_lo")
        s_qp, s_qh, s_ql = sem("q_in_psum"), sem("q_hi"), sem("q_lo")
        s_kp, s_kh, s_kl = sem("k_in_psum"), sem("k_hi"), sem("k_lo")
        s_vp, s_v = sem("v_in_psum"), sem("v_copied")
        s_halo = sem("key_halo_copied")
        s_bd = [sem("bd_loaded_0"), sem("bd_loaded_1")]
        s_S, s_R, s_RT = sem("scores_in_psum"), sem("block_maxima"), sem("maxima_transposed")
        s_nm, s_nh, s_nl = sem("neg_max"), sem("neg_max_hi"), sem("neg_max_lo")
        s_mr = [sem("mrow_loaded_0"), sem("mrow_loaded_1")]
        s_M, s_P = sem("scores_shifted"), sem("probs_ready")
        s_pv, s_rd, s_o = sem("pv_in_psum"), sem("denominators"), sem("o_ready")
        s_oTp, s_oTh, s_oTl = sem("oT_in_psum"), sem("oT_hi"), sem("oT_lo")
        s_wo, s_x2 = sem("attention_out_in_psum"), sem("x2_ready")
        s_zTp, s_zTh, s_zTl = sem("zT_in_psum"), sem("zT_hi"), sem("zT_lo")
        s_lgp, s_lg = sem("logits_in_psum"), sem("logits_ready")
        s_zst = sem("zT_stored")
        s_wG = sem("router_weights_split")
        s_lgb, s_esc = sem("biased_logits"), sem("exp_logits")
        s_rt, s_cs, s_tot = sem("routing_step"), sem("column_sums"), sem("totals_in_psum")
        s_wsel, s_wFh, s_wFl = sem("token_weights_ready"), sem("ffn_weights_hi"), sem("ffn_weights_lo")
        s_zt, s_gu, s_sg = sem("zT_loaded"), sem("gate_up_in_psum"), sem("silu_ready")
        s_hf, s_hh, s_hl = sem("hidden_ready"), sem("hidden_hi"), sem("hidden_lo")
        s_yd, s_acc, s_out = sem("ffn_out_in_psum"), sem("rows_accumulated"), sem("out_stored")

        zT_dram = nc.dram_tensor("zT_scratch", (NG, P, 2 * KT * GT), F32, kind="Internal").ap()

        def f(ap):
            return ap.bitcast(F32)

        def wait_apart(eng, s, value):
            if not isinstance(value, int):
                value = eng.to_reg(value)
                eng.wait_ge(s_w, 16)
            eng.wait_ge(s, value)

        def sweep(eng, step, prologue, epilogue):
            prologue()
            step(0, 0, 0, True, True, False)
            with eng.Fori(0, (NG - 4) // 2) as i:
                step(2 * i + 1, i, 1, False, True, False)
                step(2 * i + 2, i + 1, 0, False, True, False)
            for g in range(NG - 3, NG):
                step(g, g // 2, g % 2, False, g + 2 < NG, g == NG - 1)
            epilogue()

        XPC = NT // XC

        with nc.Block() as block:
            @block.sync
            def _(eng):
                xv = x.rearrange("(t p) d -> p t d", p=P)
                eng.dma_start(xs[:, 0:XPC, :], xv[:, 0:XPC, :]).then_inc(s_x[0], 16)
                eng.dma_start(wraw, wqkvo).then_inc(s_w, 16)
                eng.dma_start(identf[:, :], identity).then_inc(s_const, 16)
                for i in range(1, XC):
                    eng.dma_start(xs[:, i * XPC:(i + 1) * XPC, :],
                                  xv[:, i * XPC:(i + 1) * XPC, :]).then_inc(s_x[i], 16)
                eng.dma_start(graw[:, :, :], wgate).then_inc(s_const, 16)
                eng.dma_start(biasb[:, :], bias.partition_broadcast(P)).then_inc(s_const, 16)
                eng.dma_start(wfraw[:, :, :], wffn).then_inc(s_wf, 16)

                def load_bd(g, par, heads):
                    for h in heads:
                        eng.dma_start(
                            f(bd[HD * h:HD * h + HD, par, :, WIN * h:WIN * h + WIN]),
                            f(qT[HD * h:HD * h + HD, :, :, :]).rearrange("p a k (b c) -> p (a k b) c", c=WIN)
                        ).then_inc(s_bd[par], 16)

                def load_mrow(b, pb):
                    eng.wait_ge(s_nl, b + 1)
                    for hl in range(2):
                        eng.dma_start(f(mrow[hl:hl + 1, pb, :]).rearrange("o (a c) -> o a c", c=32),
                                      f(negs[:, pb, hl, :])).then_inc(s_mr[pb], 16)

                def step(g, half, par, first, more, last):
                    for n in range(BPG):
                        if not (last and n == BPG - 1):
                            load_mrow(BPG * g + n + 1, (n + 1) % 2)
                        if not last and n < 3:
                            if n == 0:
                                if first:
                                    eng.wait_ge(s_bd0, 3)
                                eng.wait_ge(s_ql, g + 2)
                                eng.wait_ge(s_qh, g + 2)
                            load_bd(g + 1, 1 - par, (range(0, 3), range(3, 6), range(6, 8))[n])
                        if not first and n == 3:
                            eng.wait_ge(s_zTl, g)
                            eng.wait_ge(s_zTh, g)
                            eng.dma_start(zT_dram[bass.ds(g - 1, 1), :, :].rearrange("o p c -> p (o c)"),
                                          f(zT[:, :, :, :]).rearrange("p a k c -> p (a k c)")).then_inc(s_zst, 16)
                            wait_apart(eng, s_zst, 16 * g)

                def prologue():
                    eng.wait_ge(s_bd0, 2)
                    eng.wait_ge(s_ql, 1)
                    eng.wait_ge(s_qh, 1)
                    load_bd(0, 0, range(8))
                    load_mrow(0, 0)

                def epilogue():
                    eng.wait_ge(s_zTl, NG)
                    eng.wait_ge(s_zTh, NG)
                    eng.dma_start(zT_dram[NG - 1], f(zT[:, :, :, :]).rearrange("p a k c -> p (a k c)")).then_inc(s_zst, 16)
                    eng.wait_ge(s_zst, 16 * NG)

                sweep(eng, step, prologue, epilogue)

                def load_zt(g):
                    eng.dma_start(f(qy[:, bass.ds(g % 2, 1), :, :, :]).rearrange("p o a k c -> p (o a k c)"),
                                  zT_dram[bass.ds(g, 1), :, :].rearrange("o p c -> p (o c)")).then_inc(s_zt, 16)
                    wait_apart(eng, s_zt, 16 * (g + 1))

                load_zt(0)
                load_zt(1)
                ov = out.rearrange("(t p) d -> p t d", p=P)
                with eng.Fori(1, NG - 1) as g:
                    eng.wait_ge(s_gu, NE * g)
                    load_zt(g + 1)
                    eng.wait_ge(s_acc, 2 * NE * g)
                    eng.dma_start(ov[:, bass.ds(TPG * (g - 1), TPG), :], xs[:, bass.ds(TPG * (g - 1), TPG), :]).then_inc(s_out, 16)
                for g in range(NG - 2, NG):
                    eng.wait_ge(s_acc, 2 * NE * (g + 1))
                    eng.dma_start(ov[:, TPG * g:TPG * (g + 1), :], xs[:, TPG * g:TPG * (g + 1), :]).then_inc(s_out, 16)
                eng.wait_ge(s_out, 16 * NG)

            @block.gpsimd
            def _(eng):
                count = [0]

                def chain(ins):
                    count[0] += 1
                    ins.then_inc(s_pool, 1)
                    eng.wait_ge(s_pool, count[0])

                chain(eng.memset(mhalf[:, :], -0.5))
                chain(eng.memset(epsb[:, :], EPS))
                chain(eng.memset(onesf[:, :], 1.0))
                chain(eng.memset(maskf[:, :, :], 0.0))
                for lo, m, q, base in ((0, 0, -1, -1), (64, 0, 1, 0), (64, 1, 1, 0)):
                    sl = maskf[lo:lo + 64, m, :]
                    chain(eng.affine_select(out=sl, in_=sl, compare_op=ALU.is_ge, fill=MASKED, base=base,
                                            pattern=[[q, WIN]], channel_multiplier=-q))
                chain(eng.memset(maskf[0:64, 1, :], MASKED))
                chain(eng.tensor_copy(window_mask[:, :], maskf[:, 0, :]))
                for g in range(NG):
                    chain(eng.tensor_copy(mask_first[:, g, :], maskf[:, 1 if g % GPB == 0 else 0, :]))
                chain(eng.memset(f(kT[:, 0, :, :, 0, :]), 0.0))
                chain(eng.memset(vt[:, :, :, :, :], 1.0))
                chain(eng.memset(vm[:, :, :, :, :], 1.0))
                eng.wait_ge(s_const, 48)
                chain(eng.tensor_copy(identb[:, :], identf[:, :]))
                eng.memset(f(ones2[:, :]), 1.0).then_inc(s_setup, 1)
                eng.wait_ge(s_setup, 1)
                eng.memset(f(bd[:, 0, 8:16, :]), 0.0).then_inc(s_bd0, 1)
                eng.wait_ge(s_bd0, 1)

                def rstd_of(which, value):
                    eng.wait_ge(s_st[which], TPG * value)
                    eng.tensor_tensor(rstd[:, which, :], mv[:, which, :, 1], epsb[:, :], ALU.add).then_inc(s_ve[which], 1)
                    eng.wait_ge(s_ve[which], value)
                    eng.tensor_tensor(rstd[:, which, :], rstd[:, which, :], mhalf[:, :], ALU.pow).then_inc(s_rs[which], 1)
                    eng.wait_ge(s_rs[which], value)

                def step(g, half, par, first, more, last):
                    if more:
                        rstd_of(0, g + 3)
                    if not first:
                        rstd_of(1, g)

                def prologue():
                    rstd_of(0, 1)
                    rstd_of(0, 2)
                    eng.wait_ge(s_bd0, 2)
                    eng.memset(f(bd[:, 1, :, :]), 0.0).then_inc(s_bd0, 1)
                    eng.wait_ge(s_bd0, 3)

                def epilogue():
                    rstd_of(1, NG)
                sweep(eng, step, prologue, epilogue)

            @block.tensor
            def _(eng):
                def product(out, lhsT, rhs, start, stop, skip=False):
                    for n, (a, b) in enumerate(((0, 0), (0, 1), (1, 0))):
                        mm = eng.matmul(out, lhsT(a), rhs(b), start=start and n == 0,
                                        stop=stop and n == 2, skip_group_check=skip)
                    return mm

                def bank(n):
                    return ps[:, n, :].rearrange("p (a c) -> p a c", a=2)

                def transposes(src, out_bank, s_done):
                    for k in range(KT):
                        for t in range(TPG):
                            mm = eng.transpose(bank(out_bank)[:, k, t * P:(t + 1) * P],
                                               src[:, t, k * P:(k + 1) * P], identf[:, :])
                    mm.then_inc(s_done, 1)

                def yT_of(G):
                    eng.wait_ge(s_yz[0], TPG * (G + 1))
                    transposes(y, BANK_B, s_yTp)

                def q_of(G):
                    eng.wait_ge(s_yTl, G + 1)
                    for m in range(KT):
                        for k in range(KT):
                            mm = product(bank(BANK_A)[:, m, :], lambda a: wA[:, a, 0, k, m * P:(m + 1) * P],
                                         lambda b: yT[:, b, k, :], k == 0, k == KT - 1)
                    mm.then_inc(s_qp, 1)

                def k_of(G):
                    eng.wait_ge(s_ql, G + 1)
                    for m in range(KT):
                        for k in range(KT):
                            mm = product(bank(BANK_A)[:, m, :], lambda a: wA[:, a, 1, k, m * P:(m + 1) * P],
                                         lambda b: yT[:, b, k, :],
                                         k == 0, k == KT - 1)
                    mm.then_inc(s_kp, 1)

                def v_of(G):
                    eng.wait_ge(s_kl, G + 1)
                    for t in range(TPG):
                        for k in range(KT):
                            mm = product(bank(BANK_A)[:, t, :], lambda a: yT[:, a, k, t * P:(t + 1) * P],
                                         lambda b: wA[:, b, 2, k, :], k == 0, k == KT - 1)
                    mm.then_inc(s_vp, 1)

                def scores_of(b, par, n, first_mask):
                    for m in range(KT):
                        product(S[n % 2][:, m, :], lambda a: kT[:, par, a, m, n:n + 2, :].rearrange("p a c -> p (a c)"),
                                lambda c: bd[:, par, (c * KT + m) * BPG + n, :], True, False)
                        mask = first_mask if n == 0 else window_mask
                        mm = eng.matmul(S[n % 2][:, m, :].rearrange("p (h q) -> p h q", q=WIN), identb[:, :],
                                        mask.to_broadcast([P, HPT, WIN]) if n == 0 else
                                        mask[:, :].unsqueeze(1).to_broadcast([P, HPT, WIN]),
                                        start=False, stop=True)
                    mm.then_inc(s_S, 1)

                def maxima_T(b, n):
                    eng.wait_ge(s_R, b + 1)
                    if n is not None:
                        eng.wait_ge(s_nm, b)
                    eng.transpose(ps[0:32, RT, 0:P], rmax[:, (n or 0) % 2, :], identf[:, :]).then_inc(s_RT, 1)

                def shift_of(b, g, n):
                    eng.wait_ge(s_mr[n % 2], 32 * (2 * g + n // 2 + 1))
                    for m in range(KT):
                        mm = eng.matmul(S[n % 2][:, m, :], ones2[:, :], mrow[:, n % 2, m * 512:(m + 1) * 512],
                                        start=False, stop=True, skip_group_check=True)
                    mm.then_inc(s_M, 1)

                def pv_of(b, par, n):
                    eng.wait_ge(s_P, b + 1)
                    v = (vm, vt)[n % 2]
                    for hp in range(HPT):
                        mm = eng.matmul(pv[:, hp, :], probs[:, n % 2, hp * P:(hp + 1) * P],
                                        v[:, par, n // 2, 2 * hp:2 * hp + 2, :].rearrange("p a c -> p (a c)"),
                                        start=True, stop=True)
                    mm.then_inc(s_pv, 1)

                def oT_of(G, par):
                    eng.wait_ge(s_o, 2 * BPG * (G + 1))
                    for n in range(BPG):
                        mm = eng.transpose(ps[:, BANK_B, n * P:(n + 1) * P], o[:, par, n, :], identf[:, :])
                    mm.then_inc(s_oTp, 1)

                def wo_of(G):
                    eng.wait_ge(s_oTl, G + 1)
                    for t in range(TPG):
                        for c in range(2):
                            mm = product(bank(BANK_B)[:, t, :], lambda a: oT[:, a, c, 2 * t:2 * t + 2, :].rearrange("p b q -> p (b q)"),
                                         lambda b: wA[:, b, 3, c, :], c == 0, c == 1)
                    mm.then_inc(s_wo, 1)

                def zT_of(G):
                    eng.wait_ge(s_x2, TPG * (G + 1))
                    eng.wait_ge(s_yz[1], TPG * (G + 1))
                    transposes(z, BANK_B, s_zTp)

                def logits_of(G):
                    eng.wait_ge(s_zTl, G + 1)
                    for t in range(TPG):
                        for k in range(KT):
                            for a in range(2):
                                mm = eng.matmul(ps[:, BANK_A, 16 * t:16 * t + 16], zT[:, a, k, t * P:(t + 1) * P],
                                                wG[:, a, k, :, :].rearrange("p a e -> p (a e)"),
                                                start=(k == 0 and a == 0), stop=(k == KT - 1 and a == 1))
                    mm.then_inc(s_lgp, 1)

                def step(g, half, par, first, more, last):
                    for n in range(BPG):
                        b = BPG * g + n
                        has_next = not (last and n == BPG - 1)
                        n2, par2 = (n + 1) % BPG, par if n < BPG - 1 else 1 - par
                        if has_next:
                            if n == BPG - 1:
                                eng.wait_ge(s_bd[par2], 128 * (half + par + 1))
                                eng.wait_ge(s_kl, g + 2)
                                eng.wait_ge(s_halo, g + 1)
                            if not (first and n == 0):
                                eng.wait_ge(s_P, b)
                            fm = mask_first[:, bass.ds(g + 1, 1), :] if n == BPG - 1 else None
                            scores_of(b + 1, par2, n2, fm)
                        shift_of(b, g, n)
                        if n == 0 and not last:
                            eng.wait_ge(s_v, g + 1)
                            q_of(g + 1)
                        if n == 1 and not last:
                            k_of(g + 1)
                        if n == 2 and not last:
                            v_of(g + 1)
                        if n == 3 and not first:
                            if not last:
                                eng.wait_ge(s_v, g + 2)
                            logits_of(g - 1)
                        if has_next:
                            maxima_T(b + 1, n2)
                        if n == 0 and not first:
                            if not last:
                                eng.wait_ge(s_yTl, g + 2)
                            oT_of(g - 1, 1 - par)
                        if n == 1 and not first:
                            wo_of(g - 1)
                        if n == 2 and not first:
                            zT_of(g - 1)
                        if n == 3 and more:
                            if not first:
                                eng.wait_ge(s_zTl, g)
                            eng.wait_ge(s_yTl, g + 2)
                            yT_of(g + 2)
                        if n == 0:
                            eng.wait_ge(s_v, g + 1)
                        if not (first and n == 0):
                            eng.wait_ge(s_o, 2 * b)
                        pv_of(b, par, n)

                def prologue():
                    eng.wait_ge(s_const, 48)
                    yT_of(0)
                    eng.wait_ge(s_wAl, 1)
                    q_of(0)
                    k_of(0)
                    v_of(0)
                    eng.wait_ge(s_yTl, 1)
                    yT_of(1)
                    eng.wait_ge(s_setup, 1)
                    eng.wait_ge(s_bd[0], 128)
                    eng.wait_ge(s_kl, 1)
                    scores_of(0, 0, 0, mask_first[:, 0:1, :])
                    maxima_T(0, None)

                def epilogue():
                    eng.wait_ge(s_zTl, NG - 1)
                    oT_of(NG - 1, 1)
                    wo_of(NG - 1)
                    zT_of(NG - 1)
                    eng.wait_ge(s_lg, NG - 1)
                    logits_of(NG - 1)
                sweep(eng, step, prologue, epilogue)

                eng.wait_ge(s_cs, 1)
                eng.matmul(ps[:, PV, 0:2 * E], onesf[:, :], wsum[:, :], start=True, stop=True).then_inc(s_tot, 1)

                def gate_up(g, e):
                    for c in range(2):
                        for k in range(KT):
                            mm = product(bank(e % 2)[:, c, :],
                                         lambda a: wF[a][:, e, (2 * c + k) * P:(2 * c + k + 1) * P],
                                         lambda b: zt_of(g, b, k), k == 0, k == KT - 1)
                    mm.then_inc(s_gu, 1)

                def down(i, e):
                    eng.wait_ge(s_hl, i + 1)
                    for t in range(TPG):
                        mm = product(bank(2 + e % 2)[:, t, :], lambda a: hh[:, e % 2, a, t * P:(t + 1) * P],
                                     lambda b: wF[b][:, e, 4 * P:6 * P], True, True)
                    mm.then_inc(s_yd, 1)

                def ffn(g, first, last):
                    for e in range(NE):
                        i = NE * g + e
                        if e < NE - 1:
                            if not (first and e == 0):
                                eng.wait_ge(s_hf, i)
                            gate_up(g, e + 1)
                        elif not last:
                            eng.wait_ge(s_zt, 16 * (g + 2))
                            eng.wait_ge(s_hf, i)
                            gate_up(g + 1, 0)
                        if not (first and e < 2):
                            eng.wait_ge(s_acc, 2 * (i - 1))
                        down(i, e)

                eng.wait_ge(s_wFl, 1)
                eng.wait_ge(s_zt, 16)
                gate_up(0, 0)
                ffn(0, True, False)
                with eng.Fori(1, NG - 1) as g:
                    ffn(g, False, False)
                ffn(NG - 1, False, True)

            @block.scalar
            def _(eng):
                def flat(ap):
                    return ap.rearrange("p a k c -> p (a k c)")

                def hi_of(dst, src_bank, s_in, s_out, G):
                    eng.wait_ge(s_in, G + 1)
                    eng.copy(dst, ps[:, src_bank, :].rearrange("p (a c) -> p a c", a=2)).then_inc(s_out, 1)

                def v_copy(G, par):
                    eng.wait_ge(s_vp, G + 1)
                    src = ps[:, BANK_A, :].rearrange("p (t h d) -> p t h d", t=TPG, h=H)
                    eng.copy(vt[:, par, :, :, 0:HD].rearrange("p t h d -> p (t h) d"),
                             src.rearrange("p t h d -> p (t h) d"))
                    eng.copy(vm[64:P, par, :, :, 0:HD].rearrange("p t h d -> p (t h) d"),
                             src[0:64].rearrange("p t h d -> p (t h) d"))
                    eng.copy(vm[0:64, par, 1, :, 0:HD], src[64:P, 0])
                    eng.copy(vm[0:64, 1 - par, 0, :, 0:HD], src[64:P, 1]).then_inc(s_v, 1)

                def k_hi(G, par):
                    hi_of(kT[:, par, 0, :, 1:BPG + 1, :].rearrange("p k b c -> p k (b c)"), BANK_A, s_kp, s_kh, G)

                def exp_of(b, n, first):
                    eng.wait_ge(s_M, b + 1)
                    if not (first and n < 2):
                        eng.wait_ge(s_pv, b - 1)
                    eng.activation(probs[:, n % 2, :], S[n % 2].rearrange("p a c -> p (a c)"), ACT.Exp,
                                   scale=HD ** -0.5).then_inc(s_P, 1)

                def step(g, half, par, first, more, last):
                    for n in range(BPG):
                        if first and n == 0:
                            eng.wait_ge(s_wAl, 1)
                        exp_of(BPG * g + n, n, first)
                        if n == 0 and not last:
                            hi_of(qT[:, 0, :, :], BANK_A, s_qp, s_qh, g + 1)
                        if n == 0 and not first:
                            eng.wait_ge(s_oTp, g)
                            eng.copy(oT[:, 0, :, :, :].rearrange("p c b q -> p b c q"),
                                     ps[:, BANK_B, :].rearrange("p (b c q) -> p b c q", b=BPG, c=2)).then_inc(s_oTh, 1)
                        if n == 1 and not last:
                            eng.wait_ge(s_kl, g + 1)
                            eng.copy(kT[:, 1 - par, :, :, 0, :].rearrange("p a k c -> p (a k) c"),
                                     f(kT[:, par, :, :, BPG, :]).rearrange("p a k c -> p (a k) c")).then_inc(s_halo, 1)
                            k_hi(g + 1, 1 - par)
                        if n == 2 and not last:
                            v_copy(g + 1, 1 - par)
                        if n == 2 and not first:
                            hi_of(zT[:, 0, :, :], BANK_B, s_zTp, s_zTh, g - 1)
                        if n == 3 and more:
                            hi_of(yT[:, 0, :, :], BANK_B, s_yTp, s_yTh, g + 2)

                def prologue():
                    eng.wait_ge(s_w, 16)
                    eng.copy(wA[:, 0, :, :, :].rearrange("p w k c -> p (w k c)"), wraw).then_inc(s_wA, 1)
                    hi_of(yT[:, 0, :, :], BANK_B, s_yTp, s_yTh, 0)
                    hi_of(qT[:, 0, :, :], BANK_A, s_qp, s_qh, 0)
                    k_hi(0, 0)
                    v_copy(0, 0)
                    hi_of(yT[:, 0, :, :], BANK_B, s_yTp, s_yTh, 1)

                def epilogue():
                    eng.wait_ge(s_oTp, NG)
                    eng.copy(oT[:, 0, :, :, :].rearrange("p c b q -> p b c q"),
                                     ps[:, BANK_B, :].rearrange("p (b c q) -> p b c q", b=BPG, c=2)).then_inc(s_oTh, 1)
                    eng.wait_ge(s_zst, 16 * (NG - 1))
                    hi_of(zT[:, 0, :, :], BANK_B, s_zTp, s_zTh, NG - 1)
                sweep(eng, step, prologue, epilogue)

                eng.wait_ge(s_lgb, 1)
                eng.activation(esc[:, :, :], logits[:, :, :], ACT.Exp, scale=-1.0).then_inc(s_esc, 1)
                eng.wait_ge(s_wf, 16)
                eng.wait_ge(s_S, BPG * NG)
                eng.copy(wF[0], wfraw[:, :, :]).then_inc(s_wFh, 1)

                def ffn(g, first):
                    for e in range(NE):
                        i = NE * g + e
                        eng.wait_ge(s_gu, i + 1)
                        if not (first and e < 2):
                            eng.wait_ge(s_hf, i - 1)
                        eng.activation(sg[:, e % 2, :], ps[:, e % 2, 0:GT], ACT.Silu).then_inc(s_sg, 1)
                        eng.wait_ge(s_hf, i + 1)
                        if not (first and e < 2):
                            eng.wait_ge(s_yd, i - 1)
                        eng.copy(hh[:, e % 2, 0, :], hf[:, e % 2, :]).then_inc(s_hh, 1)
                eng.wait_ge(s_wsel, 1)
                ffn(0, True)
                with eng.Fori(1, NG) as g:
                    ffn(g, False)

            @block.vector
            def _(eng):
                def lo_of(dst, hi, src_bank, s_in, s_out, G):
                    eng.wait_ge(s_in, G + 1)
                    eng.tensor_tensor(dst, ps[:, src_bank, :].rearrange("p (a c) -> p a c", a=2), f(hi),
                                      ALU.subtract).then_inc(s_out, 1)

                def k_lo(G, par):
                    lo_of(kT[:, par, 1, :, 1:BPG + 1, :].rearrange("p k b c -> p k (b c)"),
                          kT[:, par, 0, :, 1:BPG + 1, :].rearrange("p k b c -> p k (b c)"), BANK_A, s_kh, s_kl, G)

                def oT_lo(G):
                    eng.wait_ge(s_oTh, G + 1)
                    eng.tensor_tensor(oT[:, 1, :, :, :].rearrange("p c b q -> p b c q"),
                                      ps[:, BANK_B, :].rearrange("p (b c q) -> p b c q", b=BPG, c=2),
                                      f(oT[:, 0, :, :, :]).rearrange("p c b q -> p b c q"),
                                      ALU.subtract).then_inc(s_oTl, 1)

                def statistics(which, G):
                    for t in range(TPG):
                        eng.bn_stats(stats[:, which, t, :], xs[:, bass.ds(TPG * G + t, 1), :].rearrange("p o d -> p (o d)")
                                     ).then_inc(s_bn[which], 1)
                    for t in range(TPG):
                        wait_apart(eng, s_bn[which], TPG * G + t + 1)
                        eng.bn_aggr(mv[:, which, t, :], stats[:, which, t, :]).then_inc(s_st[which], 1)

                def normalise(which, G):
                    eng.wait_ge(s_rs[which], G + 1)
                    for t in range(TPG):
                        eng.tensor_scalar((y, z)[which][:, t, :],
                                          xs[:, bass.ds(TPG * G + t, 1), :].rearrange("p o d -> p (o d)"),
                                          mv[:, which, t, 0:1], rstd[:, which, t:t + 1], ALU.subtract, ALU.mult
                                          ).then_inc(s_yz[which], 1)

                def maxima(b, n):
                    eng.wait_ge(s_S, b + 1)
                    eng.tensor_reduce(rmax[:, n % 2, :], S[n % 2].rearrange("p a (c q) -> p (a c) q", q=32), AX.X,
                                      ALU.max, apply_transpose=True).then_inc(s_R, 1)

                def neg_max(b, n):
                    eng.wait_ge(s_RT, b + 1)
                    eng.tensor_reduce(negm[:, n % 2, :], ps[0:32, RT, 0:P].rearrange("p (g q) -> p q g", g=4), AX.X,
                                      ALU.max, negate=True).then_inc(s_nm, 1)
                    eng.wait_ge(s_nm, b + 1)
                    eng.tensor_copy(negs[:, n % 2, 0, :], negm[:, n % 2, :]).then_inc(s_nh, 1)
                    eng.wait_ge(s_nh, b + 1)
                    eng.tensor_tensor(negs[:, n % 2, 1, :], negm[:, n % 2, :], f(negs[:, n % 2, 0, :]),
                                      ALU.subtract).then_inc(s_nl, 1)

                def o_of(b, par, n):
                    eng.wait_ge(s_pv, b + 1)
                    for c in range(2):
                        sl = slice(64 * c, 64 * c + 64)
                        eng.reciprocal(rden[sl, :], pv[sl, :, VC * c + HD]).then_inc(s_rd, 1)
                    for c in range(2):
                        sl = slice(64 * c, 64 * c + 64)
                        eng.wait_ge(s_rd, 2 * b + c + 1)
                        eng.tensor_tensor(o[sl, par, n, :].rearrange("p (a d) -> p a d", d=HD),
                                          pv[sl, :, VC * c:VC * c + HD],
                                          rden[sl, :].unsqueeze(2).to_broadcast([64, HPT, HD]),
                                          ALU.mult).then_inc(s_o, 1)

                def residual(G):
                    eng.wait_ge(s_wo, G + 1)
                    for t in range(TPG):
                        xt = xs[:, bass.ds(TPG * G + t, 1), :].rearrange("p o d -> p (o d)")
                        eng.tensor_tensor(xt, xt, ps[:, BANK_B, t * D:(t + 1) * D], ALU.add).then_inc(s_x2, 1)
                    wait_apart(eng, s_x2, TPG * (G + 1))

                def logits_add(G):
                    eng.wait_ge(s_lgp, G + 1)
                    eng.tensor_reduce(logits[:, bass.ds(TPG * G, TPG), :],
                                      ps[:, BANK_A, 0:32].rearrange("p (t a e) -> p t e a", t=2, a=2), AX.X,
                                      ALU.add).then_inc(s_lg, 1)

                def step(g, half, par, first, more, last):
                    for n in range(BPG):
                        b = BPG * g + n
                        has_next = not (last and n == BPG - 1)
                        n2 = (n + 1) % BPG
                        if n == 2 and not first:
                            normalise(1, g - 1)
                        if has_next:
                            maxima(b + 1, n2)
                        if n == 0 and not last:
                            lo_of(qT[:, 1, :, :], qT[:, 0, :, :], BANK_A, s_qh, s_ql, g + 1)
                        if n == 1 and not last:
                            k_lo(g + 1, 1 - par)
                        if n == 3 and not first:
                            logits_add(g - 1)
                        if has_next:
                            neg_max(b + 1, n2)
                        if n == 0 and not first:
                            oT_lo(g - 1)
                        if n == 0 and more:
                            if first:
                                for c in range(1, XC):
                                    eng.wait_ge(s_x[c], 16)
                            statistics(0, g + 2)
                        if n == 1 and more:
                            normalise(0, g + 2)
                        if n == 1 and not first:
                            residual(g - 1)
                            statistics(1, g - 1)
                        if n == 2 and not first:
                            lo_of(zT[:, 1, :, :], zT[:, 0, :, :], BANK_B, s_zTh, s_zTl, g - 1)
                        if n == 3 and more:
                            lo_of(yT[:, 1, :, :], yT[:, 0, :, :], BANK_B, s_yTh, s_yTl, g + 2)
                        o_of(b, par, n)

                def prologue():
                    eng.memset(f(bd[:, 0, 0:8, :]), 0.0).then_inc(s_bd0, 1)
                    eng.wait_ge(s_x[0], 16)
                    statistics(0, 0)
                    normalise(0, 0)
                    statistics(0, 1)
                    eng.wait_ge(s_wA, 1)
                    eng.tensor_tensor(wA[:, 1, :, :, :].rearrange("p w k c -> p (w k c)"), wraw,
                                      f(wA[:, 0, :, :, :]).rearrange("p w k c -> p (w k c)"), ALU.subtract).then_inc(s_wAl, 1)
                    lo_of(yT[:, 1, :, :], yT[:, 0, :, :], BANK_B, s_yTh, s_yTl, 0)
                    normalise(0, 1)
                    lo_of(qT[:, 1, :, :], qT[:, 0, :, :], BANK_A, s_qh, s_ql, 0)
                    k_lo(0, 0)
                    lo_of(yT[:, 1, :, :], yT[:, 0, :, :], BANK_B, s_yTh, s_yTl, 1)
                    eng.wait_ge(s_const, 48)
                    eng.memset(f(wG[:, 1, :, 1, :]), 0.0).then_inc(s_wG, 1)
                    eng.tensor_copy(wG[:, 0, :, 0, :], graw[:, :, :]).then_inc(s_wG, 1)
                    eng.tensor_copy(wG[:, 1, :, 0, :], graw[:, :, :]).then_inc(s_wG, 1)
                    eng.wait_ge(s_wG, 3)
                    eng.tensor_tensor(wG[:, 0, :, 1, :], graw[:, :, :], f(wG[:, 0, :, 0, :]), ALU.subtract).then_inc(s_wG, 1)
                    maxima(0, 0)
                    neg_max(0, 0)

                def epilogue():
                    oT_lo(NG - 1)
                    residual(NG - 1)
                    statistics(1, NG - 1)
                    normalise(1, NG - 1)
                    lo_of(zT[:, 1, :, :], zT[:, 0, :, :], BANK_B, s_zTh, s_zTl, NG - 1)
                    logits_add(NG - 1)
                sweep(eng, step, prologue, epilogue)

                count = [0]

                def link(ins):
                    count[0] += 1
                    ins.then_inc(s_rt, 1)
                    eng.wait_ge(s_rt, count[0])

                eng.wait_ge(s_lg, NG)
                eng.wait_ge(s_setup, 1)
                eng.tensor_tensor(logits[:, :, :], logits[:, :, :], biasb[:, :].unsqueeze(1).to_broadcast([P, NT, E]),
                                  ALU.add).then_inc(s_lgb, 1)
                eng.wait_ge(s_lgb, 1)
                link(eng.memset(lt[:, :, :], 0.0))
                for e in range(1, E):
                    link(eng.memset(lt[:, e, 0:e], 1.0))
                shape = [P, NT, E, E]
                link(eng.memset(rank[:, :, :], 0.0))
                for fe in range(E):
                    other = logits[:, :, fe:fe + 1].to_broadcast([P, NT, E])
                    link(eng.tensor_tensor(cmp[:, :, :], other, logits[:, :, :], ALU.is_gt))
                    link(eng.tensor_tensor(rank[:, :, :], rank[:, :, :], cmp[:, :, :], ALU.add))
                    link(eng.tensor_tensor(cmp[:, :, :], other, logits[:, :, :], ALU.is_equal))
                    link(eng.tensor_tensor(cmp[:, :, :], cmp[:, :, :],
                                           lt[:, :, fe].unsqueeze(1).to_broadcast([P, NT, E]), ALU.mult))
                    link(eng.tensor_tensor(rank[:, :, :], rank[:, :, :], cmp[:, :, :], ALU.add))
                link(eng.tensor_scalar(rank[:, :, :], rank[:, :, :], 2.0, None, ALU.is_lt))
                eng.wait_ge(s_esc, 1)
                link(eng.tensor_scalar(esc[:, :, :], esc[:, :, :], 1.0, None, ALU.add))
                link(eng.reciprocal(esc[:, :, :], esc[:, :, :]))
                link(eng.tensor_tensor(esc[:, :, :], esc[:, :, :], rank[:, :, :], ALU.mult))
                link(eng.tensor_reduce(cmp[:, :, 0], esc[:, :, :], AX.X, ALU.add))
                link(eng.tensor_scalar(cmp[:, :, 0], cmp[:, :, 0], 1e-8, None, ALU.add))
                link(eng.reciprocal(cmp[:, :, 0], cmp[:, :, 0]))
                link(eng.tensor_tensor(esc[:, :, :], esc[:, :, :], cmp[:, :, 0:1].to_broadcast([P, NT, E]), ALU.mult))
                link(eng.tensor_reduce(wsum[:, 0:E], esc[:, :, :].rearrange("p t e -> p e t"), AX.X, ALU.add))
                eng.tensor_reduce(wsum[:, E:2 * E], rank[:, :, :].rearrange("p t e -> p e t"), AX.X,
                                  ALU.add).then_inc(s_cs, 1)
                eng.wait_ge(s_tot, 1)
                link(eng.tensor_scalar(wmean[:, :], ps[:, PV, E:2 * E], 1.0, None, ALU.max))
                link(eng.reciprocal(wmean[:, :], wmean[:, :]))
                link(eng.tensor_tensor(wmean[:, :], wmean[:, :], ps[:, PV, 0:E], ALU.mult))
                link(eng.memset(wsel[:, :, E:NE], 1.0))
                eng.tensor_tensor(wsel[:, :, 0:E], rank[:, :, :], wmean[:, :].unsqueeze(1).to_broadcast([P, NT, E]),
                                  ALU.mult).then_inc(s_wsel, 1)
                eng.wait_ge(s_wsel, 1)
                eng.wait_ge(s_wFh, 1)
                eng.tensor_tensor(wF[1], wfraw[:, :, :], f(wF[0]), ALU.subtract).then_inc(s_wFl, 1)

                def accumulate(i, g, e):
                    eng.wait_ge(s_yd, i + 1)
                    if True:
                        for t in range(TPG):
                            xt = xs[:, bass.ds(TPG * g + t, 1), :].rearrange("p o d -> p (o d)")
                            eng.scalar_tensor_tensor(
                                out=xt, in0=ps[:, 2 + e % 2, t * D:(t + 1) * D],
                                scalar=wsel[:, bass.ds(TPG * g + t, 1), e:e + 1].rearrange("p o e -> p (o e)"),
                                in1=xt, op0=ALU.mult, op1=ALU.add).then_inc(s_acc, 1)

                def ffn(g, first):
                    for e in range(NE):
                        i = NE * g + e
                        eng.wait_ge(s_sg, i + 1)
                        if not (first and e < 2):
                            eng.wait_ge(s_hl, i - 1)
                        eng.tensor_tensor(hf[:, e % 2, :], sg[:, e % 2, :], ps[:, e % 2, GT:2 * GT],
                                          ALU.mult).then_inc(s_hf, 1)
                        eng.wait_ge(s_hh, i + 1)
                        eng.tensor_tensor(hh[:, e % 2, 1, :], hf[:, e % 2, :], f(hh[:, e % 2, 0, :]),
                                          ALU.subtract).then_inc(s_hl, 1)
                        if e > 0:
                            if not (first and e == 1):
                                eng.wait_ge(s_acc, 2 * (i - 1))
                            accumulate(i - 1, g, e - 1)
                        elif not first:
                            eng.wait_ge(s_acc, 2 * (i - 1))
                            accumulate(i - 1, g - 1, NE - 1)
                ffn(0, True)
                with eng.Fori(1, NG) as g:
                    ffn(g, False)
                eng.wait_ge(s_acc, 2 * (NE * NG - 1))
                accumulate(NE * NG - 1, NG - 1, NE - 1)


def kernel(**inputs):
    import numpy as np
    import concourse.bacc as bacc
    from concourse import mybir as my
    from concourse.bass_utils import run_bass_kernel_spmd

    def transposed(w):
        return w.T.reshape(KT, P, w.shape[0]).transpose(1, 0, 2)

    a = {k: np.asarray(v) for k, v in inputs.items()}
    x = a["L0_attn_hidden"]
    wo = a["L0_attn_Wo"].T.reshape(HPT, 2, HD, D).transpose(0, 2, 1, 3).reshape(P, 2, D)
    wqkvo = np.stack([transposed(a["L0_attn_Wq"]), transposed(a["L0_attn_Wk"]), transposed(a["L0_attn_Wv"]), wo], 1)

    def expert(gate, up, down):
        return np.concatenate([transposed(gate).reshape(P, -1), transposed(up).reshape(P, -1), down.T], 1)

    ffn = [expert(a["L0_ffn_expert_gate_w"][e], a["L0_ffn_expert_up_w"][e], a["L0_ffn_expert_down_w"][e])
           for e in range(E)]
    for i in range(0, a["L0_ffn_shared_gate_w"].shape[0], EI):
        ffn.append(expert(a["L0_ffn_shared_gate_w"][i:i + EI], a["L0_ffn_shared_up_w"][i:i + EI],
                          a["L0_ffn_shared_down_w"][:, i:i + EI]))
    arrays = {
        "x": x.reshape(-1, D),
        "wqkvo": wqkvo.reshape(P, -1),
        "wgate": transposed(a["L0_ffn_gate_w"]),
        "bias": a["L0_ffn_lb_bias"],
        "wffn": np.stack(ffn, 1),
        "identity": np.eye(P, dtype=np.float32),
    }
    arrays = {k: np.ascontiguousarray(v) for k, v in arrays.items()}
    nc = bacc.Bacc("TRN2", target_bir_lowering=False, num_devices=1)
    args = [nc.dram_tensor(k, v.shape, my.dt.from_np(v.dtype), kind="ExternalInput").ap() for k, v in arrays.items()]
    args.append(nc.dram_tensor("out", arrays["x"].shape, my.dt.float32, kind="ExternalOutput").ap())
    layer(nc, *args)
    r = run_bass_kernel_spmd(nc, [arrays], core_ids=[0])
    return r.results[0]["out"].reshape(x.shape)
```

```python
from contextlib import ExitStack

import concourse.bass as bass
from concourse import mybir

F32 = mybir.dt.float32
F32R = mybir.dt.float32r
BF16 = mybir.dt.bfloat16
ALU = mybir.AluOpType
ACT = mybir.ActivationFunctionType
AX = mybir.AxisListType

P = 128
D = 256
KT = D // P
H, HD = 16, 16
WIN = 64
GT = 256
TPG = GT // P
BPG = GT // WIN
HPT = P // HD
VC = HD + 1
E = 8
EI = 128
MASKED = -1.0e30
EPS = 1e-5


def layer(nc, x, wqkvo, wgate, bias, wffn, identity, out):
    T = x.shape[0]
    NT = T // P
    NG = T // GT
    GPB = 1024 // GT
    XC = 8
    NE = wffn.shape[1]

    with ExitStack() as ctx:
        def sb(name, shape, dt=F32):
            return ctx.enter_context(nc.sbuf_tensor(name, shape, dt))

        def sem(name):
            return ctx.enter_context(nc.semaphore(name))

        xs = sb("xs", [P, NT, D])
        y = sb("y", [P, TPG, D])
        qy = sb("qy", [P, 2, 2, KT, GT], F32R)
        qT, yT = qy[:, 0, :, :, :], qy[:, 1, :, :, :]
        wA = sb("wA", [P, 2, 4, KT, D], F32R)
        bd = sb("bd", [P, 2, 2 * KT * BPG, HPT * WIN], F32R)
        kT = sb("kT", [P, 2, 2, KT, BPG + 1, WIN], F32R)
        vt = sb("vt", [P, 2, TPG, H, VC])
        vm = sb("vm", [P, 2, TPG, H, VC])
        probs = sb("probs", [P, 2, KT * HPT * WIN])
        wraw = probs[:, :, :].rearrange("p a c -> p (a c)")
        mrow = sb("mrow", [2, 2, KT * HPT * WIN], F32R)
        rmax = sb("rmax", [P, 2, 32])
        negm = sb("negm", [32, 2, 32])
        negs = sb("negs", [2 * 32, 2, 32], F32R)
        rden = sb("rden", [P, HPT])
        o = sb("o", [P, 2, BPG, P])
        oT = sb("oT", [P, 2, 2, BPG, WIN], F32R)
        z = sb("z", [P, TPG, D])
        zT = sb("zT", [P, 2, KT, GT], F32R)
        graw = sb("graw", [P, KT, E])
        wG = sb("wG", [P, 2, KT, 2, E], F32R)
        stats = sb("stats", [P, 2, TPG, 6])
        mv = sb("mv", [P, 2, TPG, 2])
        rstd = sb("rstd", [P, 2, TPG])
        mhalf, epsb = sb("mhalf", [P, TPG]), sb("epsb", [P, TPG])
        identf = sb("identf", [P, P])
        identb = sb("identb", [P, P], BF16)
        window_mask = sb("window_mask", [P, WIN], BF16)
        mask_first = sb("mask_first", [P, NG, WIN], BF16)
        maskf = sb("maskf", [P, 2, WIN])
        onesf = sb("onesf", [P, P])
        ones2 = sb("ones2", [2, P], F32R)
        logits = sb("logits", [P, NT, E])
        biasb = sb("biasb", [P, E])
        wfraw = sb("wfraw", [P, NE, 6 * P])

        bdflat = bd[:, :, :, :].rearrange("p a b c -> p (a b c)")
        wF = [bdflat[:, h * 8192:h * 8192 + NE * 6 * P].rearrange("p (e c) -> p e c", e=NE) for h in range(2)]

        ps = ctx.enter_context(nc.psum_tensor("ps", [P, 8, 512], F32))
        S = [ps[:, 2 * i:2 * i + 2, :] for i in range(2)]
        sg, hf = y, z
        hh = oT[:, :, :, :, :].rearrange("p a b c q -> p (a b c q)").rearrange("p (e a c) -> p e a c", e=2, a=2)
        esc = probs[:, 0, 0:NT * E].rearrange("p (t e) -> p t e", e=E)
        cmp = probs[:, 0, 256:256 + NT * E].rearrange("p (t e) -> p t e", e=E)
        rank = probs[:, 0, 512:512 + NT * E].rearrange("p (t e) -> p t e", e=E)

        wsel = probs[:, 1, 0:NT * NE].rearrange("p (t e) -> p t e", e=NE)
        lt = probs[:, 1, 512:512 + E * E].rearrange("p (e f) -> p e f", e=E)
        wsum, wmean = probs[:, 1, 640:640 + 2 * E], probs[:, 1, 672:672 + E]

        def zt_of(g, a, k):
            if isinstance(g, int):
                return qy[:, g % 2, a, k, :]
            return qy[:, bass.ds(g % 2, 1), a, k, :].rearrange("p o c -> p (o c)")

        PV, RT, BANK_A, BANK_B = 4, 5, 6, 7
        pv = ps[:, PV, 0:HPT * 2 * VC].rearrange("p (a b) -> p a b", a=HPT)

        s_x = [sem(f"x_loaded_{i}") for i in range(XC)]
        s_w = sem("weights_loaded")
        s_const = sem("constants_loaded")
        s_wf = sem("ffn_weights_loaded")
        s_pool = sem("pool_setup")
        s_setup = sem("constants_ready")
        s_wA = sem("attention_weights_split")
        s_wAl = sem("attention_weights_lo")
        s_bd0 = sem("bd_zeroed")
        s_bn = [sem(f"bn_stats_{i}_ready") for i in range(2)]
        s_st = [sem(f"mean_var_{i}_ready") for i in range(2)]
        s_ve = [sem(f"var_eps_{i}_ready") for i in range(2)]
        s_rs = [sem(f"rstd_{i}_ready") for i in range(2)]
        s_yz = [sem("y_ready"), sem("z_ready")]
        s_yTp, s_yTh, s_yTl = sem("yT_in_psum"), sem("yT_hi"), sem("yT_lo")
        s_qp, s_qh, s_ql = sem("q_in_psum"), sem("q_hi"), sem("q_lo")
        s_kp, s_kh, s_kl = sem("k_in_psum"), sem("k_hi"), sem("k_lo")
        s_vp, s_v = sem("v_in_psum"), sem("v_copied")
        s_halo = sem("key_halo_copied")
        s_bd = [sem("bd_loaded_0"), sem("bd_loaded_1")]
        s_S, s_R, s_RT = sem("scores_in_psum"), sem("block_maxima"), sem("maxima_transposed")
        s_nm, s_nh, s_nl = sem("neg_max"), sem("neg_max_hi"), sem("neg_max_lo")
        s_mr = [sem("mrow_loaded_0"), sem("mrow_loaded_1")]
        s_M, s_P = sem("scores_shifted"), sem("probs_ready")
        s_pv, s_rd, s_o = sem("pv_in_psum"), sem("denominators"), sem("o_ready")
        s_oTp, s_oTh, s_oTl = sem("oT_in_psum"), sem("oT_hi"), sem("oT_lo")
        s_wo, s_x2 = sem("attention_out_in_psum"), sem("x2_ready")
        s_zTp, s_zTh, s_zTl = sem("zT_in_psum"), sem("zT_hi"), sem("zT_lo")
        s_lgp, s_lg = sem("logits_in_psum"), sem("logits_ready")
        s_zst = sem("zT_stored")
        s_wG = sem("router_weights_split")
        s_lgb, s_esc = sem("biased_logits"), sem("exp_logits")
        s_rt, s_cs, s_tot = sem("routing_step"), sem("column_sums"), sem("totals_in_psum")
        s_wsel, s_wFh, s_wFl = sem("token_weights_ready"), sem("ffn_weights_hi"), sem("ffn_weights_lo")
        s_zt, s_gu, s_sg = sem("zT_loaded"), sem("gate_up_in_psum"), sem("silu_ready")
        s_hf, s_hh, s_hl = sem("hidden_ready"), sem("hidden_hi"), sem("hidden_lo")
        s_yd, s_acc, s_out = sem("ffn_out_in_psum"), sem("rows_accumulated"), sem("out_stored")

        zT_dram = nc.dram_tensor("zT_scratch", (NG, P, 2 * KT * GT), F32, kind="Internal").ap()

        def f(ap):
            return ap.bitcast(F32)

        def wait_apart(eng, s, value):
            if not isinstance(value, int):
                value = eng.to_reg(value)
                eng.wait_ge(s_w, 16)
            eng.wait_ge(s, value)

        def sweep(eng, step, prologue, epilogue):
            prologue()
            step(0, 0, 0, 0, 2)
            step(1, 0, 1, 1, 2)
            with eng.Fori(1, NG // 2 - 1) as i:
                step(2 * i, i, 0, 2, 2)
                step(2 * i + 1, i, 1, 2, 2)
            step(NG - 2, NG // 2 - 1, 0, 2, 1)
            step(NG - 1, NG // 2 - 1, 1, 2, 0)
            epilogue()

        XPC = NT // XC

        with nc.Block() as block:
            @block.sync
            def _(eng):
                xv = x.rearrange("(t p) d -> p t d", p=P)
                eng.dma_start(xs[:, 0:XPC, :], xv[:, 0:XPC, :]).then_inc(s_x[0], 16)
                eng.dma_start(wraw, wqkvo).then_inc(s_w, 16)
                eng.dma_start(identf[:, :], identity).then_inc(s_const, 16)
                for i in range(1, XC):
                    eng.dma_start(xs[:, i * XPC:(i + 1) * XPC, :],
                                  xv[:, i * XPC:(i + 1) * XPC, :]).then_inc(s_x[i], 16)
                eng.dma_start(graw[:, :, :], wgate).then_inc(s_const, 16)
                eng.dma_start(biasb[:, :], bias.partition_broadcast(P)).then_inc(s_const, 16)
                eng.dma_start(wfraw[:, :, :], wffn).then_inc(s_wf, 16)

                def load_bd(g, par, heads):
                    for h in heads:
                        eng.dma_start(
                            f(bd[HD * h:HD * h + HD, par, :, WIN * h:WIN * h + WIN]),
                            f(qT[HD * h:HD * h + HD, :, :, :]).rearrange("p a k (b c) -> p (a k b) c", c=WIN)
                        ).then_inc(s_bd[par], 16)

                def load_mrow(b, pb):
                    eng.wait_ge(s_nl, b + 1)
                    eng.dma_start(f(mrow[:, pb, :]).rearrange("h (a c) -> h a c", c=32),
                                  f(negs[:, pb, :])).then_inc(s_mr[pb], 16)

                def store_zt(G):
                    eng.wait_ge(s_zTl, G + 1)
                    eng.wait_ge(s_zTh, G + 1)
                    dst = zT_dram[G] if isinstance(G, int) else zT_dram[bass.ds(G, 1), :, :].rearrange("o p c -> p (o c)")
                    eng.dma_start(dst, f(zT[:, :, :, :]).rearrange("p a k c -> p (a k c)")).then_inc(s_zst, 16)

                def step(g, half, par, old, ahead):
                    for n in range(BPG):
                        if ahead or n < BPG - 1:
                            load_mrow(BPG * g + n + 1, (n + 1) % 2)
                        if n == 0 and ahead:
                            if old == 0:
                                eng.wait_ge(s_bd0, 3)
                            eng.wait_ge(s_ql, g + 2)
                            eng.wait_ge(s_qh, g + 2)
                            load_bd(g + 1, 1 - par, range(0, 5))
                        if n == 1 and ahead:
                            load_bd(g + 1, 1 - par, range(5, 8))
                        if n == 2 and old == 2:
                            store_zt(g - 2)

                def prologue():
                    eng.wait_ge(s_bd0, 2)
                    eng.wait_ge(s_ql, 1)
                    eng.wait_ge(s_qh, 1)
                    load_bd(0, 0, range(8))
                    load_mrow(0, 0)

                def epilogue():
                    store_zt(NG - 2)
                    store_zt(NG - 1)
                    eng.wait_ge(s_zst, 16 * NG)

                sweep(eng, step, prologue, epilogue)

                def load_zt(g):
                    eng.dma_start(f(qy[:, bass.ds(g % 2, 1), :, :, :]).rearrange("p o a k c -> p (o a k c)"),
                                  zT_dram[bass.ds(g, 1), :, :].rearrange("o p c -> p (o c)")).then_inc(s_zt, 16)
                    wait_apart(eng, s_zt, 16 * (g + 1))

                load_zt(0)
                load_zt(1)
                ov = out.rearrange("(t p) d -> p t d", p=P)
                with eng.Fori(1, NG - 1) as g:
                    eng.wait_ge(s_gu, NE * g)
                    load_zt(g + 1)
                    eng.wait_ge(s_acc, 2 * NE * g)
                    eng.dma_start(ov[:, bass.ds(TPG * (g - 1), TPG), :], xs[:, bass.ds(TPG * (g - 1), TPG), :]).then_inc(s_out, 16)
                for g in range(NG - 2, NG):
                    eng.wait_ge(s_acc, 2 * NE * (g + 1))
                    eng.dma_start(ov[:, TPG * g:TPG * (g + 1), :], xs[:, TPG * g:TPG * (g + 1), :]).then_inc(s_out, 16)
                eng.wait_ge(s_out, 16 * NG)

            @block.gpsimd
            def _(eng):
                count = [0]

                def chain(ins):
                    count[0] += 1
                    ins.then_inc(s_pool, 1)
                    eng.wait_ge(s_pool, count[0])

                chain(eng.memset(mhalf[:, :], -0.5))
                chain(eng.memset(epsb[:, :], EPS))
                chain(eng.memset(onesf[:, :], 1.0))
                chain(eng.memset(maskf[:, :, :], 0.0))
                for lo, m, q, base in ((0, 0, -1, -1), (64, 0, 1, 0), (64, 1, 1, 0)):
                    sl = maskf[lo:lo + 64, m, :]
                    chain(eng.affine_select(out=sl, in_=sl, compare_op=ALU.is_ge, fill=MASKED, base=base,
                                            pattern=[[q, WIN]], channel_multiplier=-q))
                chain(eng.memset(maskf[0:64, 1, :], MASKED))
                chain(eng.tensor_copy(window_mask[:, :], maskf[:, 0, :]))
                for g in range(NG):
                    chain(eng.tensor_copy(mask_first[:, g, :], maskf[:, 1 if g % GPB == 0 else 0, :]))
                chain(eng.memset(f(kT[:, 0, :, :, 0, :]), 0.0))
                chain(eng.memset(vt[:, :, :, :, :], 1.0))
                chain(eng.memset(vm[:, :, :, :, :], 1.0))
                eng.wait_ge(s_const, 48)
                chain(eng.tensor_copy(identb[:, :], identf[:, :]))
                eng.memset(f(ones2[:, :]), 1.0).then_inc(s_setup, 1)
                eng.wait_ge(s_setup, 1)
                eng.memset(f(bd[:, 0, 8:16, :]), 0.0).then_inc(s_bd0, 1)
                eng.wait_ge(s_bd0, 1)

                def rstd_of(which, value):
                    eng.wait_ge(s_st[which], TPG * value)
                    eng.tensor_tensor(rstd[:, which, :], mv[:, which, :, 1], epsb[:, :], ALU.add).then_inc(s_ve[which], 1)
                    eng.wait_ge(s_ve[which], value)
                    eng.tensor_tensor(rstd[:, which, :], rstd[:, which, :], mhalf[:, :], ALU.pow).then_inc(s_rs[which], 1)
                    eng.wait_ge(s_rs[which], value)

                def step(g, half, par, old, ahead):
                    if ahead == 2:
                        rstd_of(0, g + 3)
                    if old:
                        rstd_of(1, g)

                def prologue():
                    rstd_of(0, 1)
                    rstd_of(0, 2)
                    eng.wait_ge(s_bd0, 2)
                    eng.memset(f(bd[:, 1, :, :]), 0.0).then_inc(s_bd0, 1)
                    eng.wait_ge(s_bd0, 3)

                def epilogue():
                    rstd_of(1, NG)
                sweep(eng, step, prologue, epilogue)

            @block.tensor
            def _(eng):
                def product(out, lhsT, rhs, start, stop, skip=False):
                    for n, (a, b) in enumerate(((0, 0), (0, 1), (1, 0))):
                        mm = eng.matmul(out, lhsT(a), rhs(b), start=start and n == 0,
                                        stop=stop and n == 2, skip_group_check=skip)
                    return mm

                def bank(n):
                    return ps[:, n, :].rearrange("p (a c) -> p a c", a=2)

                def transposes(src, out_bank, s_done):
                    for k in range(KT):
                        for t in range(TPG):
                            mm = eng.transpose(bank(out_bank)[:, k, t * P:(t + 1) * P],
                                               src[:, t, k * P:(k + 1) * P], identf[:, :])
                    mm.then_inc(s_done, 1)

                def yT_of(G):
                    eng.wait_ge(s_yz[0], TPG * (G + 1))
                    transposes(y, BANK_A, s_yTp)

                def q_of(G):
                    eng.wait_ge(s_yTl, G + 1)
                    for m in range(KT):
                        for k in range(KT):
                            mm = product(bank(BANK_A)[:, m, :], lambda a: wA[:, a, 0, k, m * P:(m + 1) * P],
                                         lambda b: yT[:, b, k, :], k == 0, k == KT - 1)
                    mm.then_inc(s_qp, 1)

                def k_of(G):
                    eng.wait_ge(s_ql, G + 1)
                    for m in range(KT):
                        for k in range(KT):
                            mm = product(bank(BANK_A)[:, m, :], lambda a: wA[:, a, 1, k, m * P:(m + 1) * P],
                                         lambda b: yT[:, b, k, :],
                                         k == 0, k == KT - 1)
                    mm.then_inc(s_kp, 1)

                def v_of(G):
                    eng.wait_ge(s_kl, G + 1)
                    for t in range(TPG):
                        for k in range(KT):
                            mm = product(bank(BANK_A)[:, t, :], lambda a: yT[:, a, k, t * P:(t + 1) * P],
                                         lambda b: wA[:, b, 2, k, :], k == 0, k == KT - 1)
                    mm.then_inc(s_vp, 1)

                def scores_of(b, par, n, first_mask):
                    for m in range(KT):
                        product(S[n % 2][:, m, :], lambda a: kT[:, par, a, m, n:n + 2, :].rearrange("p a c -> p (a c)"),
                                lambda c: bd[:, par, (c * KT + m) * BPG + n, :], True, False)
                        mask = first_mask if n == 0 else window_mask
                        mm = eng.matmul(S[n % 2][:, m, :].rearrange("p (h q) -> p h q", q=WIN), identb[:, :],
                                        mask.to_broadcast([P, HPT, WIN]) if n == 0 else
                                        mask[:, :].unsqueeze(1).to_broadcast([P, HPT, WIN]),
                                        start=False, stop=True)
                    mm.then_inc(s_S, 1)

                def maxima_T(b, n):
                    eng.wait_ge(s_R, b + 1)
                    if n is not None:
                        eng.wait_ge(s_nm, b)
                    eng.transpose(ps[0:32, RT, 0:P], rmax[:, (n or 0) % 2, :], identf[:, :]).then_inc(s_RT, 1)

                def shift_of(b, g, n):
                    eng.wait_ge(s_mr[n % 2], 16 * (2 * g + n // 2 + 1))
                    for m in range(KT):
                        mm = eng.matmul(S[n % 2][:, m, :], ones2[:, :], mrow[:, n % 2, m * 512:(m + 1) * 512],
                                        start=False, stop=True, skip_group_check=True)
                    mm.then_inc(s_M, 1)

                def pv_of(b, par, n, wait):
                    eng.wait_ge(s_P, b + 1)
                    if wait:
                        eng.wait_ge(s_o, 2 * b)
                    v = (vm, vt)[n % 2]
                    for hp in range(HPT):
                        mm = eng.matmul(pv[:, hp, :], probs[:, n % 2, hp * P:(hp + 1) * P],
                                        v[:, par, n // 2, 2 * hp:2 * hp + 2, :].rearrange("p a c -> p (a c)"),
                                        start=True, stop=True)
                    mm.then_inc(s_pv, 1)

                def oT_of(G, par):
                    eng.wait_ge(s_o, 2 * BPG * (G + 1))
                    for n in range(BPG):
                        mm = eng.transpose(ps[:, BANK_B, n * P:(n + 1) * P], o[:, par, n, :], identf[:, :])
                    mm.then_inc(s_oTp, 1)

                def wo_of(G):
                    eng.wait_ge(s_oTl, G + 1)
                    for t in range(TPG):
                        for c in range(2):
                            mm = product(bank(BANK_B)[:, t, :], lambda a: oT[:, a, c, 2 * t:2 * t + 2, :].rearrange("p b q -> p (b q)"),
                                         lambda b: wA[:, b, 3, c, :], c == 0, c == 1)
                    mm.then_inc(s_wo, 1)

                def zT_of(G):
                    eng.wait_ge(s_x2, TPG * (G + 1))
                    eng.wait_ge(s_yz[1], TPG * (G + 1))
                    transposes(z, BANK_B, s_zTp)

                def logits_of(G):
                    eng.wait_ge(s_zTl, G + 1)
                    for t in range(TPG):
                        for k in range(KT):
                            for a in range(2):
                                mm = eng.matmul(ps[:, BANK_B, 16 * t:16 * t + 16], zT[:, a, k, t * P:(t + 1) * P],
                                                wG[:, a, k, :, :].rearrange("p a e -> p (a e)"),
                                                start=(k == 0 and a == 0), stop=(k == KT - 1 and a == 1))
                    mm.then_inc(s_lgp, 1)

                def step(g, half, par, old, ahead):
                    for n in range(BPG):
                        b = BPG * g + n
                        n2, par2 = (n + 1) % BPG, par if n < BPG - 1 else 1 - par
                        if ahead or n < BPG - 1:
                            if n == BPG - 1:
                                eng.wait_ge(s_bd[par2], 128 * (half + par + 1))
                                eng.wait_ge(s_kl, g + 2)
                                eng.wait_ge(s_halo, g + 1)
                            if old or n:
                                eng.wait_ge(s_P, b)
                            fm = mask_first[:, bass.ds(g + 1, 1), :] if n == BPG - 1 else None
                            scores_of(b + 1, par2, n2, fm)
                        if n == 1:
                            eng.wait_ge(s_v, g + 1)
                        if old or n:
                            pv_of(b - 1, 1 - par if n == 0 else par, (n - 1) % BPG, old or n > 1)
                        if ahead or n < BPG - 1:
                            maxima_T(b + 1, n2)
                        shift_of(b, g, n)
                        if n == 0:
                            if ahead:
                                q_of(g + 1)
                            if old:
                                if old == 2:
                                    eng.wait_ge(s_zTl, g - 1)
                                oT_of(g - 1, 1 - par)
                        if n == 1:
                            if ahead:
                                k_of(g + 1)
                            if old:
                                wo_of(g - 1)
                        if n == 2:
                            if ahead:
                                v_of(g + 1)
                            if old == 2:
                                eng.wait_ge(s_x2, TPG * g)
                                logits_of(g - 2)
                        if n == 3:
                            if ahead == 2:
                                eng.wait_ge(s_v, g + 2)
                                yT_of(g + 2)
                            if old:
                                if old == 2:
                                    eng.wait_ge(s_lg, g - 1)
                                zT_of(g - 1)

                def prologue():
                    eng.wait_ge(s_const, 48)
                    yT_of(0)
                    eng.wait_ge(s_wAl, 1)
                    q_of(0)
                    k_of(0)
                    v_of(0)
                    eng.wait_ge(s_v, 1)
                    yT_of(1)
                    eng.wait_ge(s_setup, 1)
                    eng.wait_ge(s_bd[0], 128)
                    eng.wait_ge(s_kl, 1)
                    scores_of(0, 0, 0, mask_first[:, 0:1, :])
                    maxima_T(0, None)

                def epilogue():
                    pv_of(BPG * NG - 1, 1, BPG - 1, True)
                    eng.wait_ge(s_zTl, NG - 1)
                    oT_of(NG - 1, 1)
                    wo_of(NG - 1)
                    eng.wait_ge(s_x2, TPG * NG)
                    logits_of(NG - 2)
                    eng.wait_ge(s_lg, NG - 1)
                    zT_of(NG - 1)
                    logits_of(NG - 1)
                sweep(eng, step, prologue, epilogue)

                eng.wait_ge(s_cs, 1)
                eng.matmul(ps[:, PV, 0:2 * E], onesf[:, :], wsum[:, :], start=True, stop=True).then_inc(s_tot, 1)

                def gate_up(g, e):
                    for c in range(2):
                        for k in range(KT):
                            mm = product(bank(e % 2)[:, c, :],
                                         lambda a: wF[a][:, e, (2 * c + k) * P:(2 * c + k + 1) * P],
                                         lambda b: zt_of(g, b, k), k == 0, k == KT - 1)
                    mm.then_inc(s_gu, 1)

                def down(i, e):
                    eng.wait_ge(s_hl, i + 1)
                    for t in range(TPG):
                        mm = product(bank(2 + e % 2)[:, t, :], lambda a: hh[:, e % 2, a, t * P:(t + 1) * P],
                                     lambda b: wF[b][:, e, 4 * P:6 * P], True, True)
                    mm.then_inc(s_yd, 1)

                def ffn(g, first, last):
                    for e in range(NE):
                        i = NE * g + e
                        if e < NE - 1:
                            if not (first and e == 0):
                                eng.wait_ge(s_hf, i)
                            gate_up(g, e + 1)
                        elif not last:
                            eng.wait_ge(s_zt, 16 * (g + 2))
                            eng.wait_ge(s_hf, i)
                            gate_up(g + 1, 0)
                        if not (first and e < 2):
                            eng.wait_ge(s_acc, 2 * (i - 1))
                        down(i, e)

                eng.wait_ge(s_wFl, 1)
                eng.wait_ge(s_zt, 16)
                gate_up(0, 0)
                ffn(0, True, False)
                with eng.Fori(1, NG - 1) as g:
                    ffn(g, False, False)
                ffn(NG - 1, False, True)

            @block.scalar
            def _(eng):
                def flat(ap):
                    return ap.rearrange("p a k c -> p (a k c)")

                def hi_of(dst, src_bank, s_in, s_out, G):
                    eng.wait_ge(s_in, G + 1)
                    eng.copy(dst, ps[:, src_bank, :].rearrange("p (a c) -> p a c", a=2)).then_inc(s_out, 1)

                def v_copy(G, par):
                    eng.wait_ge(s_vp, G + 1)
                    src = ps[:, BANK_A, :].rearrange("p (t h d) -> p t h d", t=TPG, h=H)
                    eng.copy(vt[:, par, :, :, 0:HD].rearrange("p t h d -> p (t h) d"),
                             src.rearrange("p t h d -> p (t h) d"))
                    eng.copy(vm[64:P, par, :, :, 0:HD].rearrange("p t h d -> p (t h) d"),
                             src[0:64].rearrange("p t h d -> p (t h) d"))
                    eng.copy(vm[0:64, par, 1, :, 0:HD], src[64:P, 0])
                    eng.copy(vm[0:64, 1 - par, 0, :, 0:HD], src[64:P, 1]).then_inc(s_v, 1)

                def k_hi(G, par):
                    hi_of(kT[:, par, 0, :, 1:BPG + 1, :].rearrange("p k b c -> p k (b c)"), BANK_A, s_kp, s_kh, G)

                def exp_of(b, n, first):
                    eng.wait_ge(s_M, b + 1)
                    if not (first and n < 2):
                        eng.wait_ge(s_pv, b - 1)
                    eng.activation(probs[:, n % 2, :], S[n % 2].rearrange("p a c -> p (a c)"), ACT.Exp,
                                   scale=HD ** -0.5).then_inc(s_P, 1)

                def oT_hi(G):
                    eng.wait_ge(s_oTp, G + 1)
                    eng.copy(oT[:, 0, :, :, :].rearrange("p c b q -> p b c q"),
                             ps[:, BANK_B, :].rearrange("p (b c q) -> p b c q", b=BPG, c=2)).then_inc(s_oTh, 1)

                def zT_hi(G, stored):
                    if stored:
                        eng.wait_ge(s_zst, 16 * G)
                    hi_of(zT[:, 0, :, :], BANK_B, s_zTp, s_zTh, G)

                def step(g, half, par, old, ahead):
                    for n in range(BPG):
                        if old == 0 and n == 0:
                            eng.wait_ge(s_wAl, 1)
                        exp_of(BPG * g + n, n, old == 0)
                        if n == 0 and ahead:
                            hi_of(qT[:, 0, :, :], BANK_A, s_qp, s_qh, g + 1)
                        if n == 0 and old:
                            oT_hi(g - 1)
                        if n == 1 and ahead:
                            eng.wait_ge(s_kl, g + 1)
                            eng.copy(kT[:, 1 - par, :, :, 0, :].rearrange("p a k c -> p (a k) c"),
                                     f(kT[:, par, :, :, BPG, :]).rearrange("p a k c -> p (a k) c")).then_inc(s_halo, 1)
                            k_hi(g + 1, 1 - par)
                        if n == 2 and ahead:
                            v_copy(g + 1, 1 - par)
                        if n == 3 and ahead == 2:
                            hi_of(yT[:, 0, :, :], BANK_A, s_yTp, s_yTh, g + 2)
                        if n == 3 and old:
                            zT_hi(g - 1, old == 2)

                def prologue():
                    eng.wait_ge(s_w, 16)
                    eng.copy(wA[:, 0, :, :, :].rearrange("p w k c -> p (w k c)"), wraw).then_inc(s_wA, 1)
                    hi_of(yT[:, 0, :, :], BANK_A, s_yTp, s_yTh, 0)
                    hi_of(qT[:, 0, :, :], BANK_A, s_qp, s_qh, 0)
                    k_hi(0, 0)
                    v_copy(0, 0)
                    hi_of(yT[:, 0, :, :], BANK_A, s_yTp, s_yTh, 1)

                def epilogue():
                    oT_hi(NG - 1)
                    zT_hi(NG - 1, True)
                sweep(eng, step, prologue, epilogue)

                eng.wait_ge(s_lgb, 1)
                eng.activation(esc[:, :, :], logits[:, :, :], ACT.Exp, scale=-1.0).then_inc(s_esc, 1)
                eng.wait_ge(s_wf, 16)
                eng.wait_ge(s_S, BPG * NG)
                eng.copy(wF[0], wfraw[:, :, :]).then_inc(s_wFh, 1)

                def ffn(g, first):
                    for e in range(NE):
                        i = NE * g + e
                        eng.wait_ge(s_gu, i + 1)
                        if not (first and e < 2):
                            eng.wait_ge(s_hf, i - 1)
                        eng.activation(sg[:, e % 2, :], ps[:, e % 2, 0:GT], ACT.Silu).then_inc(s_sg, 1)
                        eng.wait_ge(s_hf, i + 1)
                        if not (first and e < 2):
                            eng.wait_ge(s_yd, i - 1)
                        eng.copy(hh[:, e % 2, 0, :], hf[:, e % 2, :]).then_inc(s_hh, 1)
                eng.wait_ge(s_wsel, 1)
                ffn(0, True)
                with eng.Fori(1, NG) as g:
                    ffn(g, False)

            @block.vector
            def _(eng):
                def lo_of(dst, hi, src_bank, s_in, s_out, G):
                    eng.wait_ge(s_in, G + 1)
                    eng.tensor_tensor(dst, ps[:, src_bank, :].rearrange("p (a c) -> p a c", a=2), f(hi),
                                      ALU.subtract).then_inc(s_out, 1)

                def k_lo(G, par):
                    lo_of(kT[:, par, 1, :, 1:BPG + 1, :].rearrange("p k b c -> p k (b c)"),
                          kT[:, par, 0, :, 1:BPG + 1, :].rearrange("p k b c -> p k (b c)"), BANK_A, s_kh, s_kl, G)

                def oT_lo(G):
                    eng.wait_ge(s_oTh, G + 1)
                    eng.tensor_tensor(oT[:, 1, :, :, :].rearrange("p c b q -> p b c q"),
                                      ps[:, BANK_B, :].rearrange("p (b c q) -> p b c q", b=BPG, c=2),
                                      f(oT[:, 0, :, :, :]).rearrange("p c b q -> p b c q"),
                                      ALU.subtract).then_inc(s_oTl, 1)

                def statistics(which, G):
                    for t in range(TPG):
                        eng.bn_stats(stats[:, which, t, :], xs[:, bass.ds(TPG * G + t, 1), :].rearrange("p o d -> p (o d)")
                                     ).then_inc(s_bn[which], 1)
                    for t in range(TPG):
                        wait_apart(eng, s_bn[which], TPG * G + t + 1)
                        eng.bn_aggr(mv[:, which, t, :], stats[:, which, t, :]).then_inc(s_st[which], 1)

                def normalise(which, G):
                    eng.wait_ge(s_rs[which], G + 1)
                    for t in range(TPG):
                        eng.tensor_scalar((y, z)[which][:, t, :],
                                          xs[:, bass.ds(TPG * G + t, 1), :].rearrange("p o d -> p (o d)"),
                                          mv[:, which, t, 0:1], rstd[:, which, t:t + 1], ALU.subtract, ALU.mult
                                          ).then_inc(s_yz[which], 1)

                def maxima(b, n):
                    eng.wait_ge(s_S, b + 1)
                    eng.tensor_reduce(rmax[:, n % 2, :], S[n % 2].rearrange("p a (c q) -> p (a c) q", q=32), AX.X,
                                      ALU.max, apply_transpose=True).then_inc(s_R, 1)

                def neg_max(b, n):
                    eng.wait_ge(s_RT, b + 1)
                    eng.tensor_reduce(negm[:, n % 2, :], ps[0:32, RT, 0:P].rearrange("p (g q) -> p q g", g=4), AX.X,
                                      ALU.max, negate=True).then_inc(s_nm, 1)
                    eng.wait_ge(s_nm, b + 1)
                    eng.tensor_copy(negs[0:32, n % 2, :], negm[:, n % 2, :]).then_inc(s_nh, 1)
                    eng.wait_ge(s_nh, b + 1)
                    eng.tensor_tensor(negs[32:64, n % 2, :], negm[:, n % 2, :], f(negs[0:32, n % 2, :]),
                                      ALU.subtract).then_inc(s_nl, 1)

                def o_of(b, par, n):
                    eng.wait_ge(s_pv, b + 1)
                    for c in range(2):
                        sl = slice(64 * c, 64 * c + 64)
                        eng.reciprocal(rden[sl, :], pv[sl, :, VC * c + HD]).then_inc(s_rd, 1)
                    for c in range(2):
                        sl = slice(64 * c, 64 * c + 64)
                        eng.wait_ge(s_rd, 2 * b + c + 1)
                        eng.tensor_tensor(o[sl, par, n, :].rearrange("p (a d) -> p a d", d=HD),
                                          pv[sl, :, VC * c:VC * c + HD],
                                          rden[sl, :].unsqueeze(2).to_broadcast([64, HPT, HD]),
                                          ALU.mult).then_inc(s_o, 1)

                def residual(G):
                    eng.wait_ge(s_wo, G + 1)
                    for t in range(TPG):
                        xt = xs[:, bass.ds(TPG * G + t, 1), :].rearrange("p o d -> p (o d)")
                        eng.tensor_tensor(xt, xt, ps[:, BANK_B, t * D:(t + 1) * D], ALU.add).then_inc(s_x2, 1)
                    wait_apart(eng, s_x2, TPG * (G + 1))

                def logits_add(G):
                    eng.wait_ge(s_lgp, G + 1)
                    eng.tensor_reduce(logits[:, bass.ds(TPG * G, TPG), :],
                                      ps[:, BANK_B, 0:32].rearrange("p (t a e) -> p t e a", t=2, a=2), AX.X,
                                      ALU.add).then_inc(s_lg, 1)

                def step(g, half, par, old, ahead):
                    for n in range(BPG):
                        b = BPG * g + n
                        n2 = (n + 1) % BPG
                        if ahead or n < BPG - 1:
                            maxima(b + 1, n2)
                        if n == 2 and old:
                            residual(g - 1)
                        if n == 3 and old:
                            normalise(1, g - 1)
                        if ahead or n < BPG - 1:
                            neg_max(b + 1, n2)
                        if old or n:
                            o_of(b - 1, par if n else 1 - par, (n - 1) % BPG)
                        if n == 0:
                            if ahead:
                                lo_of(qT[:, 1, :, :], qT[:, 0, :, :], BANK_A, s_qh, s_ql, g + 1)
                            if ahead == 2:
                                if old == 0:
                                    for c in range(1, XC):
                                        eng.wait_ge(s_x[c], 16)
                                statistics(0, g + 2)
                            if old:
                                oT_lo(g - 1)
                        if n == 1:
                            if ahead:
                                k_lo(g + 1, 1 - par)
                            if ahead == 2:
                                normalise(0, g + 2)
                        if n == 2:
                            if old:
                                statistics(1, g - 1)
                            if old == 2:
                                logits_add(g - 2)
                        if n == 3:
                            if ahead == 2:
                                lo_of(yT[:, 1, :, :], yT[:, 0, :, :], BANK_A, s_yTh, s_yTl, g + 2)
                            if old:
                                lo_of(zT[:, 1, :, :], zT[:, 0, :, :], BANK_B, s_zTh, s_zTl, g - 1)

                def prologue():
                    eng.memset(f(bd[:, 0, 0:8, :]), 0.0).then_inc(s_bd0, 1)
                    eng.wait_ge(s_x[0], 16)
                    statistics(0, 0)
                    normalise(0, 0)
                    statistics(0, 1)
                    eng.wait_ge(s_wA, 1)
                    eng.tensor_tensor(wA[:, 1, :, :, :].rearrange("p w k c -> p (w k c)"), wraw,
                                      f(wA[:, 0, :, :, :]).rearrange("p w k c -> p (w k c)"), ALU.subtract).then_inc(s_wAl, 1)
                    lo_of(yT[:, 1, :, :], yT[:, 0, :, :], BANK_A, s_yTh, s_yTl, 0)
                    normalise(0, 1)
                    lo_of(qT[:, 1, :, :], qT[:, 0, :, :], BANK_A, s_qh, s_ql, 0)
                    k_lo(0, 0)
                    lo_of(yT[:, 1, :, :], yT[:, 0, :, :], BANK_A, s_yTh, s_yTl, 1)
                    eng.wait_ge(s_const, 48)
                    eng.memset(f(wG[:, 1, :, 1, :]), 0.0).then_inc(s_wG, 1)
                    eng.tensor_copy(wG[:, 0, :, 0, :], graw[:, :, :]).then_inc(s_wG, 1)
                    eng.tensor_copy(wG[:, 1, :, 0, :], graw[:, :, :]).then_inc(s_wG, 1)
                    eng.wait_ge(s_wG, 3)
                    eng.tensor_tensor(wG[:, 0, :, 1, :], graw[:, :, :], f(wG[:, 0, :, 0, :]), ALU.subtract).then_inc(s_wG, 1)
                    maxima(0, 0)
                    neg_max(0, 0)

                def epilogue():
                    o_of(BPG * NG - 1, 1, BPG - 1)
                    oT_lo(NG - 1)
                    residual(NG - 1)
                    statistics(1, NG - 1)
                    logits_add(NG - 2)
                    normalise(1, NG - 1)
                    lo_of(zT[:, 1, :, :], zT[:, 0, :, :], BANK_B, s_zTh, s_zTl, NG - 1)
                    logits_add(NG - 1)
                sweep(eng, step, prologue, epilogue)

                count = [0]

                def link(ins):
                    count[0] += 1
                    ins.then_inc(s_rt, 1)
                    eng.wait_ge(s_rt, count[0])

                eng.wait_ge(s_lg, NG)
                eng.wait_ge(s_setup, 1)
                eng.tensor_tensor(logits[:, :, :], logits[:, :, :], biasb[:, :].unsqueeze(1).to_broadcast([P, NT, E]),
                                  ALU.add).then_inc(s_lgb, 1)
                eng.wait_ge(s_lgb, 1)
                link(eng.memset(lt[:, :, :], 0.0))
                for e in range(1, E):
                    link(eng.memset(lt[:, e, 0:e], 1.0))
                shape = [P, NT, E, E]
                link(eng.memset(rank[:, :, :], 0.0))
                for fe in range(E):
                    other = logits[:, :, fe:fe + 1].to_broadcast([P, NT, E])
                    link(eng.tensor_tensor(cmp[:, :, :], other, logits[:, :, :], ALU.is_gt))
                    link(eng.tensor_tensor(rank[:, :, :], rank[:, :, :], cmp[:, :, :], ALU.add))
                    link(eng.tensor_tensor(cmp[:, :, :], other, logits[:, :, :], ALU.is_equal))
                    link(eng.tensor_tensor(cmp[:, :, :], cmp[:, :, :],
                                           lt[:, :, fe].unsqueeze(1).to_broadcast([P, NT, E]), ALU.mult))
                    link(eng.tensor_tensor(rank[:, :, :], rank[:, :, :], cmp[:, :, :], ALU.add))
                link(eng.tensor_scalar(rank[:, :, :], rank[:, :, :], 2.0, None, ALU.is_lt))
                eng.wait_ge(s_esc, 1)
                link(eng.tensor_scalar(esc[:, :, :], esc[:, :, :], 1.0, None, ALU.add))
                link(eng.reciprocal(esc[:, :, :], esc[:, :, :]))
                link(eng.tensor_tensor(esc[:, :, :], esc[:, :, :], rank[:, :, :], ALU.mult))
                link(eng.tensor_reduce(cmp[:, :, 0], esc[:, :, :], AX.X, ALU.add))
                link(eng.tensor_scalar(cmp[:, :, 0], cmp[:, :, 0], 1e-8, None, ALU.add))
                link(eng.reciprocal(cmp[:, :, 0], cmp[:, :, 0]))
                link(eng.tensor_tensor(esc[:, :, :], esc[:, :, :], cmp[:, :, 0:1].to_broadcast([P, NT, E]), ALU.mult))
                link(eng.tensor_reduce(wsum[:, 0:E], esc[:, :, :].rearrange("p t e -> p e t"), AX.X, ALU.add))
                eng.tensor_reduce(wsum[:, E:2 * E], rank[:, :, :].rearrange("p t e -> p e t"), AX.X,
                                  ALU.add).then_inc(s_cs, 1)
                eng.wait_ge(s_tot, 1)
                link(eng.tensor_scalar(wmean[:, :], ps[:, PV, E:2 * E], 1.0, None, ALU.max))
                link(eng.reciprocal(wmean[:, :], wmean[:, :]))
                link(eng.tensor_tensor(wmean[:, :], wmean[:, :], ps[:, PV, 0:E], ALU.mult))
                link(eng.memset(wsel[:, :, E:NE], 1.0))
                eng.tensor_tensor(wsel[:, :, 0:E], rank[:, :, :], wmean[:, :].unsqueeze(1).to_broadcast([P, NT, E]),
                                  ALU.mult).then_inc(s_wsel, 1)
                eng.wait_ge(s_wsel, 1)
                eng.wait_ge(s_wFh, 1)
                eng.tensor_tensor(wF[1], wfraw[:, :, :], f(wF[0]), ALU.subtract).then_inc(s_wFl, 1)

                def accumulate(i, g, e):
                    eng.wait_ge(s_yd, i + 1)
                    if True:
                        for t in range(TPG):
                            xt = xs[:, bass.ds(TPG * g + t, 1), :].rearrange("p o d -> p (o d)")
                            eng.scalar_tensor_tensor(
                                out=xt, in0=ps[:, 2 + e % 2, t * D:(t + 1) * D],
                                scalar=wsel[:, bass.ds(TPG * g + t, 1), e:e + 1].rearrange("p o e -> p (o e)"),
                                in1=xt, op0=ALU.mult, op1=ALU.add).then_inc(s_acc, 1)

                def ffn(g, first):
                    for e in range(NE):
                        i = NE * g + e
                        eng.wait_ge(s_sg, i + 1)
                        if not (first and e < 2):
                            eng.wait_ge(s_hl, i - 1)
                        eng.tensor_tensor(hf[:, e % 2, :], sg[:, e % 2, :], ps[:, e % 2, GT:2 * GT],
                                          ALU.mult).then_inc(s_hf, 1)
                        eng.wait_ge(s_hh, i + 1)
                        eng.tensor_tensor(hh[:, e % 2, 1, :], hf[:, e % 2, :], f(hh[:, e % 2, 0, :]),
                                          ALU.subtract).then_inc(s_hl, 1)
                        if e > 0:
                            if not (first and e == 1):
                                eng.wait_ge(s_acc, 2 * (i - 1))
                            accumulate(i - 1, g, e - 1)
                        elif not first:
                            eng.wait_ge(s_acc, 2 * (i - 1))
                            accumulate(i - 1, g - 1, NE - 1)
                ffn(0, True)
                with eng.Fori(1, NG) as g:
                    ffn(g, False)
                eng.wait_ge(s_acc, 2 * (NE * NG - 1))
                accumulate(NE * NG - 1, NG - 1, NE - 1)


def kernel(**inputs):
    import numpy as np
    import concourse.bacc as bacc
    from concourse import mybir as my
    from concourse.bass_utils import run_bass_kernel_spmd

    def transposed(w):
        return w.T.reshape(KT, P, w.shape[0]).transpose(1, 0, 2)

    a = {k: np.asarray(v) for k, v in inputs.items()}
    x = a["L0_attn_hidden"]
    wo = a["L0_attn_Wo"].T.reshape(HPT, 2, HD, D).transpose(0, 2, 1, 3).reshape(P, 2, D)
    wqkvo = np.stack([transposed(a["L0_attn_Wq"]), transposed(a["L0_attn_Wk"]), transposed(a["L0_attn_Wv"]), wo], 1)

    def expert(gate, up, down):
        return np.concatenate([transposed(gate).reshape(P, -1), transposed(up).reshape(P, -1), down.T], 1)

    ffn = [expert(a["L0_ffn_expert_gate_w"][e], a["L0_ffn_expert_up_w"][e], a["L0_ffn_expert_down_w"][e])
           for e in range(E)]
    for i in range(0, a["L0_ffn_shared_gate_w"].shape[0], EI):
        ffn.append(expert(a["L0_ffn_shared_gate_w"][i:i + EI], a["L0_ffn_shared_up_w"][i:i + EI],
                          a["L0_ffn_shared_down_w"][:, i:i + EI]))
    arrays = {
        "x": x.reshape(-1, D),
        "wqkvo": wqkvo.reshape(P, -1),
        "wgate": transposed(a["L0_ffn_gate_w"]),
        "bias": a["L0_ffn_lb_bias"],
        "wffn": np.stack(ffn, 1),
        "identity": np.eye(P, dtype=np.float32),
    }
    arrays = {k: np.ascontiguousarray(v) for k, v in arrays.items()}
    nc = bacc.Bacc("TRN2", target_bir_lowering=False, num_devices=1)
    args = [nc.dram_tensor(k, v.shape, my.dt.from_np(v.dtype), kind="ExternalInput").ap() for k, v in arrays.items()]
    args.append(nc.dram_tensor("out", arrays["x"].shape, my.dt.float32, kind="ExternalOutput").ap())
    layer(nc, *args)
    r = run_bass_kernel_spmd(nc, [arrays], core_ids=[0])
    return r.results[0]["out"].reshape(x.shape)
```

```python
from contextlib import ExitStack

import concourse.bass as bass
from concourse import mybir

F32 = mybir.dt.float32
F32R = mybir.dt.float32r
I32 = mybir.dt.int32
BF16 = mybir.dt.bfloat16
ALU = mybir.AluOpType
ACT = mybir.ActivationFunctionType
AX = mybir.AxisListType

P = 128
D = 256
KT = D // P
H, HD = 16, 16
WIN = 64
GT = 256
TPG = GT // P
BPG = GT // WIN
HPT = P // HD
VC = HD + 1
E = 8
EI = 128
MASKED = -1.0e30
EPS = 1e-5
K = 2
ZR = D + 2


def expert_tiles(T):
    return -(-((K * T + E * (P - 1)) // P) // 8) * 8


def constants(T):
    at, c = {}, 0
    for name, n in (("token", T // P), ("before", P), ("region", E), ("expert", E), ("lower", E * E),
                    ("upto", E * E), ("tile_rows", T // P), ("tile", expert_tiles(T)), ("choice", K)):
        at[name] = (c, n)
        c += n
    return at, c


def layer(nc, x, wqkvo, wgate, bias, wffn, identity, consts, out):
    T = x.shape[0]
    NT = T // P
    NG = T // GT
    GPB = 1024 // GT
    XC = 8
    NS = wffn.shape[1] - E
    NTS = expert_tiles(T)
    REGION = T + P
    GA = 7
    EW = 4
    at, NCONST = constants(T)

    with ExitStack() as ctx:
        def sb(name, shape, dt=F32):
            return ctx.enter_context(nc.sbuf_tensor(name, shape, dt))

        def sem(name):
            return ctx.enter_context(nc.semaphore(name))

        def f(ap):
            return ap.bitcast(F32)

        xs = sb("xs", [P, NT, D])
        y = sb("y", [P, TPG, D])
        qy = sb("qy", [P, 2, 2, KT, GT], F32R)
        qT, yT = qy[:, 0, :, :, :], qy[:, 1, :, :, :]
        wA = sb("wA", [P, 2, 4, KT, D], F32R)
        bd = sb("bd", [P, 2, 2 * KT * BPG, HPT * WIN], F32R)
        kT = sb("kT", [P, 2, 2, KT, BPG + 1, WIN], F32R)
        vt = sb("vt", [P, 2, TPG, H, VC])
        vm = sb("vm", [P, 2, TPG, H, VC])
        probs = sb("probs", [P, 2, KT * HPT * WIN])
        wraw = probs[:, :, :].rearrange("p a c -> p (a c)")
        mrow = sb("mrow", [2, 2, KT * HPT * WIN], F32R)
        rmax = sb("rmax", [P, 2, 32])
        negm = sb("negm", [32, 2, 32])
        negs = sb("negs", [2 * 32, 2, 32], F32R)
        rden = sb("rden", [P, HPT])
        o = sb("o", [P, 2, BPG, P])
        oT = sb("oT", [P, 2, 2, BPG, WIN], F32R)
        z = sb("z", [P, 2, TPG, ZR])
        zT = sb("zT", [P, 2, KT, GT], F32R)
        graw = sb("graw", [P, KT, E])
        wG = sb("wG", [P, 2, KT, 2, E], F32R)
        stats = sb("stats", [P, 2, TPG, 6])
        mv = sb("mv", [P, 2, TPG, 2])
        rstd = sb("rstd", [P, 2, TPG])
        mhalf, epsb = sb("mhalf", [P, TPG]), sb("epsb", [P, TPG])
        identf = sb("identf", [P, P])
        identb = sb("identb", [P, P], BF16)
        window_mask = sb("window_mask", [P, WIN], BF16)
        mask_first = sb("mask_first", [P, GPB, WIN], BF16)
        onesf = sb("onesf", [P, P])
        ones2 = sb("ones2", [2, P], F32R)
        logits = sb("logits", [P, NT, E])
        biasb = sb("biasb", [P, E])
        wfraw = sb("wfraw", [P, NS + EW, 6 * P])
        cst = sb("cst", [P, NCONST])
        before = sb("before", [P, P], BF16)
        onesb = sb("onesb", [P, P], BF16)
        cmp_gt, cmp_eq = sb("cmp_gt", [P, TPG, E, E]), sb("cmp_eq", [P, TPG, E, E])
        maskf = cmp_gt[:, :, :, :].rearrange("p t e f -> p (t e f)").rearrange("p (m q) -> p m q", q=WIN)
        rank = sb("rank", [P, TPG, E])
        chosen = sb("chosen", [P, K, TPG, E])
        sel = sb("sel", [P, NT, E], BF16)
        seen = sb("seen", [P, E], BF16)
        slots = sb("slots", [P, TPG, E])
        slot_of = sb("slot_of", [P, K, TPG, E])
        slot_f = sb("slot_f", [P, K, TPG])
        slot = sb("slot", [P, 2, K, TPG], I32)
        fill = sb("fill", [P, ZR])
        fill_at = sb("fill_at", [P, E], I32)
        counts = sb("counts", [P, 4, E])
        tile_e, tile_w = sb("tile_e", [P, NTS]), sb("tile_w", [P, NTS])
        tile_ei, tile_row = sb("tile_ei", [P, NTS + 2], I32), sb("tile_row", [P, NTS], I32)
        zin = sb("zin", [P, 4, ZR])
        h1 = sb("h1", [P, 2, 2, P])
        dest_f, dest = sb("dest_f", [P, 4]), sb("dest", [P, 4], I32)

        bdflat = bd[:, :, :, :].rearrange("p a b c -> p (a b c)")
        wF = [bdflat[:, h * 8192:h * 8192 + (E + NS) * 6 * P].rearrange("p (e c) -> p e c", e=E + NS) for h in range(2)]
        wAflat = wA[:, :, :, :, :].rearrange("p a w k c -> p (a w k c)")
        raw_of = [wfraw[:, NS + e, :] for e in range(EW)] + [
            f(wAflat[:, c:c + 6 * P]) for c in (0, 6 * P, 2048, 2048 + 6 * P)]
        z1 = wAflat[:, 0:2 * 2 * D].rearrange("p (b a c) -> p b a c", b=2, a=2)
        hT = wAflat[:, 2048:2048 + 2 * 2 * P].rearrange("p (b a c) -> p b a c", b=2, a=2)

        ps = ctx.enter_context(nc.psum_tensor("ps", [P, 8, 512], F32))
        S = [ps[:, 2 * i:2 * i + 2, :] for i in range(2)]
        yo = wfraw[:, :, :].rearrange("p e c -> p (e c)")[:, 0:4 * D].rearrange("p (b c) -> p b c", b=4)
        hf = o[:, 0, :, :].rearrange("p b c -> p (b c)").rearrange("p (e c) -> p e c", e=2)
        sg = y
        hh = [bdflat[:, 8192 * e + 7680:8192 * (e + 1)].rearrange("p (a c) -> p a c", a=2) for e in range(NS)]
        ya = [v[:, :, :, :, :].rearrange("p a t h c -> p (a t h c)")[:, 0:K * TPG * D].rearrange(
            "p (j t d) -> p j t d", j=K, t=TPG) for v in (vt, vm)]
        ya += [wfraw[:, :, :].rearrange("p e c -> p (e c)")[:, c:c + K * TPG * D].rearrange(
            "p (j t d) -> p j t d", j=K, t=TPG) for c in (4 * D, 4 * D + K * TPG * D)]
        table = [probs[:, i, 0:NTS * E].rearrange("p (t e) -> p t e", e=E) for i in range(2)]
        esc = probs[:, 0, 640:640 + NT * E].rearrange("p (t e) -> p t e", e=E)
        token_sum = probs[:, 0, 896:896 + NT]
        wsum = probs[:, 1, 640:640 + E]
        few = probs[:, 1, 704:704 + E * NT].rearrange("p (e k) -> p e k", e=E)

        def const(name):
            return cst[:, at[name][0]:at[name][0] + at[name][1]]

        kTflat = kT[:, :, :, :, :, :].rearrange("p a b k c q -> p (a b k c q)")
        s_zt = [sem(f"zT_loaded_{i}") for i in range(5)]
        zt_places = [qy[:, 0], qy[:, 1]] + [flat[:, c:c + 2 * KT * GT].rearrange("p (a k c) -> p a k c", a=2, k=KT)
                                            for flat, c in ((kTflat, 0), (kTflat, 1024), (wAflat, 3072))]
        zt_order = [g % 2 for g in range(GA)] + [(g - GA) % 5 for g in range(GA, NG)]
        zt_of = [(zt_places[n], s_zt[n], 16 * (zt_order[:g].count(n) + 1)) for g, n in enumerate(zt_order)]

        PV, RT, BANK_A, BANK_B = 4, 5, 6, 7
        pv = ps[:, PV, 0:HPT * 2 * VC].rearrange("p (a b) -> p a b", a=HPT)

        s_x = [sem(f"x_loaded_{i}") for i in range(XC)]
        s_w2 = sem("weights_vo_loaded")
        s_w = sem("weights_loaded")
        s_id, s_const = sem("identity_loaded"), sem("constants_loaded")
        s_wcp = sem("weights_copied")
        s_wf2 = sem("last_experts_weights_loaded")
        s_wf = sem("ffn_weights_loaded")
        s_pool = sem("pool_setup")
        s_setup = sem("constants_ready")
        s_v1 = sem("ones_beside_v")
        s_wA = sem("attention_weights_split")
        s_wAl = sem("attention_weights_lo")
        s_bd0 = sem("bd_zeroed")
        s_bn = [sem(f"bn_stats_{i}_ready") for i in range(2)]
        s_st = [sem(f"mean_var_{i}_ready") for i in range(2)]
        s_ve = [sem(f"var_eps_{i}_ready") for i in range(2)]
        s_rs = [sem(f"rstd_{i}_ready") for i in range(2)]
        s_yz = [sem("y_ready"), sem("z_ready")]
        s_yTp, s_yTh, s_yTl = sem("yT_in_psum"), sem("yT_hi"), sem("yT_lo")
        s_qp, s_qh, s_ql = sem("q_in_psum"), sem("q_hi"), sem("q_lo")
        s_kp, s_kh, s_kl = sem("k_in_psum"), sem("k_hi"), sem("k_lo")
        s_vp, s_v = sem("v_in_psum"), sem("v_copied")
        s_halo = sem("key_halo_copied")
        s_bd = [sem("bd_loaded_0"), sem("bd_loaded_1")]
        s_S, s_R, s_RT = sem("scores_in_psum"), sem("block_maxima"), sem("maxima_transposed")
        s_nm, s_nh, s_nl = sem("neg_max"), sem("neg_max_hi"), sem("neg_max_lo")
        s_mr = [sem("mrow_loaded_0"), sem("mrow_loaded_1")]
        s_M, s_P = sem("scores_shifted"), sem("probs_ready")
        s_pv, s_rd, s_o = sem("pv_in_psum"), sem("denominators"), sem("o_ready")
        s_oTp, s_oTh, s_oTl = sem("oT_in_psum"), sem("oT_hi"), sem("oT_lo")
        s_wo, s_x2 = sem("attention_out_in_psum"), sem("x2_ready")
        s_zTp, s_zTh, s_zTl = sem("zT_in_psum"), sem("zT_hi"), sem("zT_lo")
        s_lgp, s_lg = sem("logits_in_psum"), sem("logits_ready")
        s_zst = sem("zT_stored")
        s_tok = sem("tokens_numbered")
        s_rk, s_cum, s_sl, s_ix, s_sc = (sem("ranking_step"), sem("places_in_psum"), sem("slot_step"),
                                         sem("slots_ready"), sem("rows_scattered"))
        s_cnt, s_fo, s_fill, s_tab, s_tw = (sem("counts_in_psum"), sem("fill_places"), sem("tiles_filled"),
                                            sem("tile_table"), sem("tile_weights"))
        s_zin, s_ysc = [sem(f"rows_loaded_{i}") for i in range(4)], [sem(f"rows_out_{i}") for i in range(4)]
        s_T, s_zh, s_zl = sem("rows_transposed"), sem("rows_hi"), sem("rows_lo")
        s_g1, s_s1, s_h1 = sem("tile_gate_up"), sem("tile_silu"), sem("tile_hidden")
        s_hT, s_hTh, s_hTl = sem("hidden_transposed"), sem("hiddenT_hi"), sem("hiddenT_lo")
        s_d1, s_y1, s_ds, s_df = sem("tile_out"), sem("tile_scaled"), sem("tile_places"), sem("tile_places_float")
        s_ya = [sem(f"expert_rows_{i}") for i in range(4)]
        s_yy, s_cb = sem("expert_rows_together"), sem("expert_rows_added")
        s_wG = sem("router_weights_split")
        s_esc = sem("router_scores")
        s_rt, s_cs, s_tot = sem("routing_step"), sem("column_sums"), sem("totals_in_psum")
        s_wSh, s_wSl = sem("shared_weights_hi"), sem("shared_weights_lo")
        s_wFh, s_wFl = sem("expert_weights_hi"), sem("expert_weights_lo")
        s_gu, s_sg = sem("gate_up_in_psum"), sem("silu_ready")
        s_hf, s_hh, s_hl = sem("hidden_ready"), sem("hidden_hi"), sem("hidden_lo")
        s_yd, s_acc, s_out = sem("ffn_out_in_psum"), sem("rows_accumulated"), sem("out_stored")

        w_copy = nc.dram_tensor("w_copy", (P, E - EW, 6 * P), F32, kind="Internal").ap()
        z_slots = nc.dram_tensor("z_slots", (E * REGION + P, ZR), F32, kind="Internal").ap()
        y_rows = nc.dram_tensor("y_rows", (K * T, D), F32, kind="Internal").ap()
        zT_dram = nc.dram_tensor("zT_scratch", (NG, P, 2 * KT * GT), F32, kind="Internal").ap()

        def wait_apart(eng, s, value):
            if not isinstance(value, int):
                value = eng.to_reg(value)
                eng.wait_ge(s_w, 16)
            eng.wait_ge(s, value)

        def after(eng, s, value):
            if not isinstance(value, int) or value > 0:
                eng.wait_ge(s, value)

        def sweep(eng, step, prologue, epilogue):
            prologue()
            for g in range(4):
                step(g, g // 2, g % 2, min(g, 3), 2)
            with eng.Fori(2, NG // 2 - 1) as i:
                step(2 * i, i, 0, 3, 2)
                step(2 * i + 1, i, 1, 3, 2)
            step(NG - 2, NG // 2 - 1, 0, 3, 1)
            step(NG - 1, NG // 2 - 1, 1, 3, 0)
            epilogue()

        def sweep_tiles(eng, tile, begin=None):
            def eight(q, first, last):
                if begin:
                    begin(q)
                for m in range(8):
                    tile(q, m, first, last)
            eight(0, True, False)
            with eng.Fori(1, NTS // 8 - 1) as q:
                eight(q, False, False)
            eight(NTS // 8 - 1, False, True)

        def later(q, m, d):
            return 8 * q + m + d, 2 * q + (m + d) // 4, (m + d) % 4

        XPC = NT // XC

        with nc.Block() as block:
            @block.sync
            def _(eng):
                xv = x.rearrange("(t p) d -> p t d", p=P)
                eng.dma_start(xs[:, 0:XPC, :], xv[:, 0:XPC, :]).then_inc(s_x[0], 16)
                eng.dma_start(identf[:, :], identity).then_inc(s_id, 16)
                eng.dma_start(wraw[:, 0:1024], wqkvo[:, 0:1024]).then_inc(s_w, 16)
                eng.dma_start(wraw[:, 1024:2048], wqkvo[:, 1024:2048]).then_inc(s_w2, 16)
                eng.dma_start(graw[:, :, :], wgate).then_inc(s_const, 16)
                eng.dma_start(biasb[:, :], bias.partition_broadcast(P)).then_inc(s_const, 16)
                eng.dma_start(cst[:, :], consts).then_inc(s_const, 16)
                def load_x(i):
                    eng.dma_start(xs[:, i * XPC:(i + 1) * XPC, :],
                                  xv[:, i * XPC:(i + 1) * XPC, :]).then_inc(s_x[i], 16)

                for i in range(1, XC):
                    load_x(i)
                eng.dma_start(wfraw[:, 0:NS, :], wffn[:, E:E + NS, :]).then_inc(s_wf, 16)
                for e in range(EW):
                    eng.dma_start(wfraw[:, NS + e, :], wffn[:, e, :]).then_inc(s_wf, 16)

                def load_in_step(g, n):
                    if g in (2, 3) and n >= 2:
                        c = 2 * (g - 2) + n - 2
                        eng.dma_start(w_copy[:, c, :], wffn[:, EW + c, :]).then_inc(s_wcp, 16)

                def load_bd(g, par, heads):
                    for h in heads:
                        eng.dma_start(
                            f(bd[HD * h:HD * h + HD, par, :, WIN * h:WIN * h + WIN]),
                            f(qT[HD * h:HD * h + HD, :, :, :]).rearrange("p a k (b c) -> p (a k b) c", c=WIN)
                        ).then_inc(s_bd[par], 16)

                def load_mrow(b, pb):
                    eng.wait_ge(s_nl, b + 1)
                    eng.dma_start(f(mrow[:, pb, :]).rearrange("h (a c) -> h a c", c=32),
                                  f(negs[:, pb, :])).then_inc(s_mr[pb], 16)

                def store_zt(G):
                    eng.wait_ge(s_zTl, G + 1)
                    eng.wait_ge(s_zTh, G + 1)
                    dst = zT_dram[G] if isinstance(G, int) else zT_dram[bass.ds(G, 1), :, :].rearrange("o p c -> p (o c)")
                    eng.dma_start(dst, f(zT[:, :, :, :]).rearrange("p a k c -> p (a k c)")).then_inc(s_zst, 16)

                def step(g, half, par, old, ahead):
                    for n in range(BPG):
                        if ahead or n < BPG - 1:
                            load_mrow(BPG * g + n + 1, (n + 1) % 2)
                        if isinstance(g, int):
                            load_in_step(g, n)
                        if ahead == 0:
                            eng.wait_ge(s_vp, NG)
                            eng.wait_ge(s_wcp, 16 * (E - EW))
                            eng.dma_start(raw_of[EW + n], w_copy[:, n, :]).then_inc(s_wf2, 16)
                        if n == 0 and ahead:
                            if old == 0:
                                eng.wait_ge(s_bd0, 3)
                            eng.wait_ge(s_ql, g + 2)
                            eng.wait_ge(s_qh, g + 2)
                            load_bd(g + 1, 1 - par, range(0, 5))
                        if n == 1 and ahead:
                            load_bd(g + 1, 1 - par, range(5, 8))
                        if n == 2 and old >= 2:
                            store_zt(g - 2)

                def prologue():
                    eng.wait_ge(s_bd0, 2)
                    eng.wait_ge(s_ql, 1)
                    eng.wait_ge(s_qh, 1)
                    load_bd(0, 0, range(8))
                    load_mrow(0, 0)

                def epilogue():
                    eng.wait_ge(s_S, BPG * NG)
                    eng.wait_ge(s_zst, 32)
                    for g in range(2):
                        eng.dma_start(f(qy[:, g, :, :, :]).rearrange("p a k c -> p (a k c)"), zT_dram[g]).then_inc(s_zt[g], 16)
                    store_zt(NG - 2)
                    store_zt(NG - 1)
                    eng.wait_ge(s_zst, 16 * NG)

                sweep(eng, step, prologue, epilogue)

                eng.wait_ge(s_setup, 1)
                eng.wait_ge(s_fo, 1)
                for e in range(E):
                    row = eng.value_load(fill_at[0:1, e:e + 1], min_val=0, max_val=E * REGION - P)
                    eng.dma_start(z_slots[bass.ds(row, P), :], fill[:, :]).then_inc(s_fill, 16)
                eng.dma_start(z_slots[E * REGION:E * REGION + P, :], fill[:, :]).then_inc(s_fill, 16)

                eng.wait_ge(s_fill, 16 * (E + 1))
                eng.wait_ge(s_sc, 64 * NG)
                eng.wait_ge(s_tab, 1)
                row_regs = [eng.alloc_register(f"row_{m}") for m in range(8)]

                def rows_of(q):
                    eng.load(row_regs, tile_row[0:1, bass.ds(8 * q, 8)])

                def load_rows(q8, m8, first, last):
                    t, q, m = later(q8, m8, 0)
                    row = eng.snap(row_regs[m8], min_val=0, max_val=E * REGION)
                    read = (t - 3, 2 * (t - 3)) if isinstance(t, int) else (eng.to_reg(t - 3), eng.to_reg(2 * (t - 3)))
                    after(eng, s_T, read[0])
                    after(eng, s_df, read[1])
                    eng.dma_start(zin[:, m, :], z_slots[bass.ds(row, P), :]).then_inc(s_zin[m], 16)
                sweep_tiles(eng, load_rows, rows_of)

                yv = y_rows.rearrange("(j t p) d -> p j t d", p=P, j=K)
                ov = out.rearrange("(t p) d -> p t d", p=P)

                def load_experts_rows(g, par):
                    for j in range(K):
                        eng.dma_start(ya[par][:, j, :, :], yv[:, j, bass.ds(TPG * g, TPG), :]).then_inc(s_ya[par], 16)

                for m in range(4):
                    eng.wait_ge(s_ysc[m], 16 * (NTS // 4))
                for g in range(4):
                    load_experts_rows(g, g)

                def store_out(g, m, more):
                    eng.wait_ge(s_cb, g + 1)
                    eng.dma_start(ov[:, bass.ds(TPG * g, TPG), :], xs[:, bass.ds(TPG * g, TPG), :]).then_inc(s_out, 16)
                    if more:
                        load_experts_rows(g + 4, m)
                with eng.Fori(0, NG // 4 - 1) as q:
                    for m in range(4):
                        store_out(4 * q + m, m, True)
                for m in range(4):
                    store_out(NG - 4 + m, m, False)
                eng.wait_ge(s_out, 16 * NG)

            @block.gpsimd
            def _(eng):
                count = [0]

                def chain(ins):
                    count[0] += 1
                    ins.then_inc(s_pool, 1)
                    eng.wait_ge(s_pool, count[0])

                chain(eng.memset(mhalf[:, :], -0.5))
                chain(eng.memset(epsb[:, :], EPS))
                def rstd_of(which, value):
                    eng.wait_ge(s_st[which], TPG * value)
                    eng.tensor_tensor(rstd[:, which, :], mv[:, which, :, 1], epsb[:, :], ALU.add).then_inc(s_ve[which], 1)
                    eng.wait_ge(s_ve[which], value)
                    eng.tensor_tensor(rstd[:, which, :], rstd[:, which, :], mhalf[:, :], ALU.pow).then_inc(s_rs[which], 1)
                    eng.wait_ge(s_rs[which], value)

                rstd_of(0, 1)
                eng.memset(f(bd[:, 0, 0:8, :]), 0.0).then_inc(s_bd0, 1)
                eng.wait_ge(s_bd0, 1)
                rstd_of(0, 2)
                eng.memset(f(bd[:, 0, 8:16, :]), 0.0).then_inc(s_bd0, 1)
                eng.wait_ge(s_bd0, 2)
                chain(eng.memset(onesf[:, :], 1.0))
                chain(eng.memset(maskf[:, :, :], 0.0))
                for lo, m, q, base in ((0, 0, -1, -1), (64, 0, 1, 0), (64, 1, 1, 0)):
                    sl = maskf[lo:lo + 64, m, :]
                    chain(eng.affine_select(out=sl, in_=sl, compare_op=ALU.is_ge, fill=MASKED, base=base,
                                            pattern=[[q, WIN]], channel_multiplier=-q))
                chain(eng.memset(maskf[0:64, 1, :], MASKED))
                chain(eng.tensor_copy(window_mask[:, :], maskf[:, 0, :]))
                for g in range(GPB):
                    chain(eng.tensor_copy(mask_first[:, g, :], maskf[:, 0 if g else 1, :]))
                eng.wait_ge(s_id, 16)
                eng.wait_ge(s_const, 48)
                chain(eng.tensor_copy(identb[:, :], identf[:, :]))
                chain(eng.tensor_copy(before[:, :], const("before")))
                chain(eng.memset(onesb[:, :], 1.0))
                chain(eng.memset(seen[:, :], 0.0))
                chain(eng.memset(fill[:, 0:D], 0.0))
                chain(eng.memset(fill[:, D:D + 1], 1.0 * K * T))
                chain(eng.memset(fill[:, D + 1:D + 2], -1.0))
                eng.memset(f(ones2[:, :]), 1.0).then_inc(s_setup, 1)
                eng.wait_ge(s_setup, 1)

                def scatter(G, par):
                    wait_apart(eng, s_ix, G + 1)
                    for t in range(TPG):
                        for j in range(K):
                            eng.indirect_dma_start(z_slots, bass.IndirectOffsetOnAxis(ap=slot[:, par, j, t:t + 1], axis=0),
                                                   z[:, par, t, :], None, bounds_check=E * REGION - 1,
                                                   oob_is_err=False).then_inc(s_sc, 16)

                def step(g, half, par, old, ahead):
                    if ahead == 2:
                        rstd_of(0, g + 3)
                    if old == 3:
                        scatter(g - 3, 1 - par)
                    if old:
                        rstd_of(1, g)

                def prologue():
                    eng.memset(f(bd[:, 1, :, :]), 0.0).then_inc(s_bd0, 1)
                    eng.wait_ge(s_bd0, 3)

                def expert_lo(e):
                    eng.wait_ge(s_wFh, e + 1)
                    eng.tensor_tensor(wF[1][:, e, :], raw_of[e], f(wF[0][:, e, :]), ALU.subtract).then_inc(s_wFl, 1)
                    eng.wait_ge(s_wFl, e + 1)

                def epilogue():
                    scatter(NG - 3, 1)
                    expert_lo(0)
                    expert_lo(1)
                    rstd_of(1, NG)
                    expert_lo(2)
                    expert_lo(3)
                    scatter(NG - 2, 0)
                    expert_lo(4)
                    scatter(NG - 1, 1)
                    for e in range(5, E):
                        expert_lo(e)
                sweep(eng, step, prologue, epilogue)

                def rows_out(q8, m8, first, last):
                    t, q, m = later(q8, m8, 0)
                    wait_apart(eng, s_y1, t + 1)
                    wait_apart(eng, s_ds, t + 1)
                    eng.indirect_dma_start(y_rows, bass.IndirectOffsetOnAxis(ap=dest[:, m:m + 1], axis=0),
                                           yo[:, m, :], None, bounds_check=K * T - 1, oob_is_err=False
                                           ).then_inc(s_ysc[m], 16)
                sweep_tiles(eng, rows_out)

                def combine(q, m):
                    wait_apart(eng, s_ya[m], 16 * K * (q + 1))
                    eng.tensor_tensor(ya[m][:, 0, :, :], ya[m][:, 0, :, :], ya[m][:, 1, :, :], ALU.add).then_inc(s_yy, 1)
                with eng.Fori(0, NG // 4) as q:
                    for m in range(4):
                        combine(q, m)

            @block.tensor
            def _(eng):
                def product(out, lhsT, rhs, start, stop, skip=False):
                    for n, (a, b) in enumerate(((0, 0), (0, 1), (1, 0))):
                        mm = eng.matmul(out, lhsT(a), rhs(b), start=start and n == 0,
                                        stop=stop and n == 2, skip_group_check=skip)
                    return mm

                def bank(n):
                    return ps[:, n, :].rearrange("p (a c) -> p a c", a=2)

                def transposes(src, out_bank, s_done):
                    for k in range(KT):
                        for t in range(TPG):
                            mm = eng.transpose(bank(out_bank)[:, k, t * P:(t + 1) * P],
                                               src[:, t, k * P:(k + 1) * P], identf[:, :])
                    mm.then_inc(s_done, 1)

                def yT_of(G):
                    eng.wait_ge(s_yz[0], TPG * (G + 1))
                    transposes(y, BANK_A, s_yTp)

                def q_of(G):
                    eng.wait_ge(s_yTl, G + 1)
                    for m in range(KT):
                        for k in range(KT):
                            mm = product(bank(BANK_A)[:, m, :], lambda a: wA[:, a, 0, k, m * P:(m + 1) * P],
                                         lambda b: yT[:, b, k, :], k == 0, k == KT - 1)
                    mm.then_inc(s_qp, 1)

                def k_of(G, to=BANK_A):
                    if to == BANK_A:
                        eng.wait_ge(s_ql, G + 1)
                    for m in range(KT):
                        for k in range(KT):
                            mm = product(bank(to)[:, m, :], lambda a: wA[:, a, 1, k, m * P:(m + 1) * P],
                                         lambda b: yT[:, b, k, :],
                                         k == 0, k == KT - 1)
                    mm.then_inc(s_kp, 1)

                def v_of(G, read=s_kl):
                    eng.wait_ge(read, G + 1)
                    for t in range(TPG):
                        for k in range(KT):
                            mm = product(bank(BANK_A)[:, t, :], lambda a: yT[:, a, k, t * P:(t + 1) * P],
                                         lambda b: wA[:, b, 2, k, :], k == 0, k == KT - 1)
                    mm.then_inc(s_vp, 1)

                def scores_of(b, par, n, first_mask):
                    for m in range(KT):
                        product(S[n % 2][:, m, :], lambda a: kT[:, par, a, m, n:n + 2, :].rearrange("p a c -> p (a c)"),
                                lambda c: bd[:, par, (c * KT + m) * BPG + n, :], True, False)
                        mask = first_mask if n == 0 else window_mask
                        mm = eng.matmul(S[n % 2][:, m, :].rearrange("p (h q) -> p h q", q=WIN), identb[:, :],
                                        mask.to_broadcast([P, HPT, WIN]) if n == 0 else
                                        mask[:, :].unsqueeze(1).to_broadcast([P, HPT, WIN]),
                                        start=False, stop=True)
                    mm.then_inc(s_S, 1)

                def maxima_T(b, n):
                    eng.wait_ge(s_R, b + 1)
                    if n is not None:
                        eng.wait_ge(s_nm, b)
                    eng.transpose(ps[0:32, RT, 0:P], rmax[:, (n or 0) % 2, :], identf[:, :]).then_inc(s_RT, 1)

                def shift_of(b, g, n):
                    eng.wait_ge(s_mr[n % 2], 16 * (2 * g + n // 2 + 1))
                    for m in range(KT):
                        mm = eng.matmul(S[n % 2][:, m, :], ones2[:, :], mrow[:, n % 2, m * 512:(m + 1) * 512],
                                        start=False, stop=True, skip_group_check=True)
                    mm.then_inc(s_M, 1)

                def pv_of(b, par, n, wait):
                    eng.wait_ge(s_P, b + 1)
                    if wait:
                        eng.wait_ge(s_o, 2 * b)
                    v = (vm, vt)[n % 2]
                    for hp in range(HPT):
                        mm = eng.matmul(pv[:, hp, :], probs[:, n % 2, hp * P:(hp + 1) * P],
                                        v[:, par, n // 2, 2 * hp:2 * hp + 2, :].rearrange("p a c -> p (a c)"),
                                        start=True, stop=True)
                    mm.then_inc(s_pv, 1)

                def oT_of(G, par):
                    eng.wait_ge(s_o, 2 * BPG * (G + 1))
                    for n in range(BPG):
                        mm = eng.transpose(ps[:, BANK_B, n * P:(n + 1) * P], o[:, par, n, :], identf[:, :])
                    mm.then_inc(s_oTp, 1)

                def wo_of(G):
                    eng.wait_ge(s_oTl, G + 1)
                    for t in range(TPG):
                        for c in range(2):
                            mm = product(bank(BANK_B)[:, t, :], lambda a: oT[:, a, c, 2 * t:2 * t + 2, :].rearrange("p b q -> p (b q)"),
                                         lambda b: wA[:, b, 3, c, :], c == 0, c == 1)
                    mm.then_inc(s_wo, 1)

                def zT_of(G, par):
                    eng.wait_ge(s_x2, TPG * (G + 1))
                    eng.wait_ge(s_yz[1], TPG * (G + 1))
                    transposes(z[:, par], BANK_B, s_zTp)

                def logits_of(G):
                    eng.wait_ge(s_zTl, G + 1)
                    for t in range(TPG):
                        for k in range(KT):
                            for a in range(2):
                                mm = eng.matmul(ps[:, BANK_B, 16 * t:16 * t + 16], zT[:, a, k, t * P:(t + 1) * P],
                                                wG[:, a, k, :, :].rearrange("p a e -> p (a e)"),
                                                start=(k == 0 and a == 0), stop=(k == KT - 1 and a == 1))
                    mm.then_inc(s_lgp, 1)

                def places_of(G):
                    eng.wait_ge(s_rk, 10 * G + 8)
                    one = [sel[:, bass.ds(TPG * G + t, 1), :].rearrange("p o e -> p (o e)") for t in range(TPG)]
                    out = [ps[:, RT, 256 + E * t:256 + E * (t + 1)] for t in range(TPG)]
                    eng.matmul(out[0], before[:, :], one[0], start=True, stop=False)
                    eng.matmul(out[0], onesb[:, :], seen[:, :], start=False, stop=True)
                    eng.matmul(out[1], before[:, :], one[1], start=True, stop=False)
                    eng.matmul(out[1], onesb[:, :], one[0], start=False, stop=False)
                    eng.matmul(out[1], onesb[:, :], seen[:, :], start=False, stop=True).then_inc(s_cum, 1)

                def step(g, half, par, old, ahead):
                    for n in range(BPG):
                        b = BPG * g + n
                        n2, par2 = (n + 1) % BPG, par if n < BPG - 1 else 1 - par
                        if ahead or n < BPG - 1:
                            if n == BPG - 1:
                                eng.wait_ge(s_bd[par2], 128 * (half + par + 1))
                                eng.wait_ge(s_kl, g + 2)
                                eng.wait_ge(s_halo, g + 1)
                            if old or n:
                                eng.wait_ge(s_P, b)
                            fm = mask_first[:, bass.ds((g + 1) % GPB, 1), :] if n == BPG - 1 else None
                            scores_of(b + 1, par2, n2, fm)
                        if n == 1:
                            eng.wait_ge(s_v, g + 1)
                        if old or n:
                            pv_of(b - 1, 1 - par if n == 0 else par, (n - 1) % BPG, old or n > 1)
                        if n == 2 and old == 3:
                            eng.wait_ge(s_ix, g - 2)
                        if ahead or n < BPG - 1:
                            maxima_T(b + 1, n2)
                        shift_of(b, g, n)
                        if n == 0:
                            if ahead:
                                q_of(g + 1)
                            if old:
                                if old >= 2:
                                    eng.wait_ge(s_zTl, g - 1)
                                oT_of(g - 1, 1 - par)
                        if n == 1:
                            if ahead:
                                k_of(g + 1)
                            if old:
                                wo_of(g - 1)
                            if old == 3:
                                eng.wait_ge(s_nm, b + 2)
                                places_of(g - 3)
                        if n == 2:
                            if ahead:
                                v_of(g + 1)
                            if old >= 2:
                                eng.wait_ge(s_x2, TPG * g)
                                logits_of(g - 2)
                        if n == 3:
                            if ahead == 2:
                                eng.wait_ge(s_v, g + 2)
                                yT_of(g + 2)
                            if old:
                                if old >= 2:
                                    eng.wait_ge(s_lg, g - 1)
                                zT_of(g - 1, 1 - par)

                def prologue():
                    eng.wait_ge(s_id, 16)
                    yT_of(0)
                    eng.wait_ge(s_wAl, 1)
                    q_of(0)
                    k_of(0, BANK_B)
                    eng.wait_ge(s_wAl, 2)
                    v_of(0, s_ql)
                    eng.wait_ge(s_v, 1)
                    yT_of(1)
                    eng.wait_ge(s_setup, 1)
                    eng.wait_ge(s_bd[0], 128)
                    eng.wait_ge(s_kl, 1)
                    scores_of(0, 0, 0, mask_first[:, 0:1, :])
                    maxima_T(0, None)

                def gate_up(i):
                    g, e = i // NS, i % NS
                    if e == 0:
                        eng.wait_ge(zt_of[g][1], zt_of[g][2])
                    after(eng, s_hf, i - 1)
                    for c in range(2):
                        for k in range(KT):
                            mm = product(bank(e)[:, c, :],
                                         lambda a: wF[a][:, E + e, (2 * k + c) * P:(2 * k + c + 1) * P],
                                         lambda b: zt_of[g][0][:, b, k, :], k == 0, k == KT - 1)
                    mm.then_inc(s_gu, 1)

                def down(i):
                    e = i % NS
                    eng.wait_ge(s_hl, i + 1)
                    after(eng, s_acc, i - 1)
                    for t in range(TPG):
                        mm = product(bank(2 + e)[:, t, :], lambda a: hh[e][:, a, t * P:(t + 1) * P],
                                     lambda b: wF[b][:, E + e, 4 * P:6 * P], True, True)
                    mm.then_inc(s_yd, 1)

                def epilogue():
                    eng.wait_ge(s_nm, BPG * NG)
                    places_of(NG - 3)
                    pv_of(BPG * NG - 1, 1, BPG - 1, True)
                    eng.wait_ge(s_wSl, 1)
                    gate_up(0)
                    eng.wait_ge(s_zTl, NG - 1)
                    oT_of(NG - 1, 1)
                    gate_up(1)
                    wo_of(NG - 1)
                    down(0)
                    eng.wait_ge(s_x2, TPG * NG)
                    logits_of(NG - 2)
                    gate_up(2)
                    eng.wait_ge(s_lg, NG - 1)
                    zT_of(NG - 1, 1)
                    eng.wait_ge(s_ix, NG - 2)
                    places_of(NG - 2)
                    down(1)
                    gate_up(3)
                    logits_of(NG - 1)
                    down(2)
                    gate_up(4)
                    eng.wait_ge(s_ix, NG - 1)
                    places_of(NG - 1)
                    down(3)
                    gate_up(5)
                    eng.wait_ge(s_ix, NG)
                    eng.matmul(ps[:, RT, 288:288 + E], onesb[:, :], seen[:, :], start=True, stop=True).then_inc(s_cnt, 1)
                sweep(eng, step, prologue, epilogue)

                for i in range(4, NS * GA - 2):
                    down(i)
                    gate_up(i + 2)
                    if i == 9:
                        eng.wait_ge(s_cs, 1)
                        eng.matmul(ps[:, BANK_B, 0:E], onesf[:, :], wsum, start=True, stop=True).then_inc(s_tot, 1)

                expert_regs = [eng.alloc_register(f"expert_{m}") for m in range(10)]

                def experts_of(q):
                    eng.load(expert_regs, tile_ei[0:1, bass.ds(8 * q, 10)])

                def weights(e, a, c0, c1):
                    return wF[a][:, bass.ds(e, 1), c0:c1].rearrange("p o c -> p (o c)")

                def rows_T(t, q, m):
                    eng.wait_ge(s_zin[m], 16 * (q + 1))
                    after(eng, s_zl, t - 1)
                    for k in range(KT):
                        mm = eng.transpose(ps[:, 4 + m % 2, k * P:(k + 1) * P], zin[:, m, k * P:(k + 1) * P], identf[:, :])
                    mm.then_inc(s_T, 1)

                def tile_gate_up(t, q, m, reg):
                    e = eng.snap(expert_regs[reg], min_val=0, max_val=E - 1)
                    eng.wait_ge(s_zl, t + 1)
                    after(eng, s_h1, t - 1)
                    for k in range(KT):
                        mm = product(ps[:, m % 2, 0:2 * P], lambda a: z1[:, m % 2, a, k * P:(k + 1) * P],
                                     lambda b: weights(e, b, 2 * k * P, 2 * (k + 1) * P), k == 0, k == KT - 1)
                    mm.then_inc(s_g1, 1)

                def hidden_T(t, q, m):
                    eng.wait_ge(s_h1, t + 1)
                    if isinstance(t, int) and t == 1:
                        eng.wait_ge(s_tw, 1)
                    after(eng, s_hTl, t - 1)
                    eng.transpose(ps[:, 6 + m % 2, 0:P], h1[:, m % 2, 1, :], identf[:, :]).then_inc(s_hT, 1)

                def tile_down(t, q, m, reg):
                    e = eng.snap(expert_regs[reg], min_val=0, max_val=E - 1)
                    eng.wait_ge(s_hTl, t + 1)
                    if isinstance(t, int) and t < 2:
                        eng.wait_ge(s_acc, NS * GA - 1 + t)
                    after(eng, s_y1, t - 1)
                    product(ps[:, 2 + m % 2, 0:D], lambda a: hT[:, m % 2, a, :],
                            lambda b: weights(e, b, 4 * P, 6 * P), True, True).then_inc(s_d1, 1)

                def tile(q, m, first, last):
                    if not (last and m >= 6):
                        rows_T(*later(q, m, 2))
                    if not (last and m == 7):
                        tile_gate_up(*later(q, m, 1), m + 2)
                    hidden_T(*later(q, m, 0))
                    if not (first and m == 0):
                        tile_down(*later(q, m, -1), m)
                rows_T(0, 0, 0)
                rows_T(1, 0, 1)
                down(NS * GA - 2)
                eng.wait_ge(s_wFl, E)
                experts_of(0)
                tile_gate_up(0, 0, 0, 1)
                down(NS * GA - 1)
                eng.wait_ge(s_hf, NS * GA)
                sweep_tiles(eng, tile, experts_of)
                eng.wait_ge(s_h1, NTS)
                gate_up(NS * GA)
                tile_down(NTS - 1, NTS // 4 - 1, 3, 8)
                eng.wait_ge(s_y1, NTS)
                for i in range(NS * GA, NS * NG):
                    if i + 1 < NS * NG:
                        gate_up(i + 1)
                    down(i)

            @block.scalar
            def _(eng):
                def flat(ap):
                    return ap.rearrange("p a k c -> p (a k c)")

                def hi_of(dst, src_bank, s_in, s_out, G):
                    eng.wait_ge(s_in, G + 1)
                    eng.copy(dst, ps[:, src_bank, :].rearrange("p (a c) -> p a c", a=2)).then_inc(s_out, 1)

                def v_copy(G, par):
                    if isinstance(G, int) and G == 0:
                        eng.wait_ge(s_v1, 3)
                    eng.wait_ge(s_vp, G + 1)
                    src = ps[:, BANK_A, :].rearrange("p (t h d) -> p t h d", t=TPG, h=H)
                    eng.copy(vt[:, par, :, :, 0:HD].rearrange("p t h d -> p (t h) d"),
                             src.rearrange("p t h d -> p (t h) d"))
                    eng.copy(vm[64:P, par, :, :, 0:HD].rearrange("p t h d -> p (t h) d"),
                             src[0:64].rearrange("p t h d -> p (t h) d"))
                    eng.copy(vm[0:64, par, 1, :, 0:HD], src[64:P, 0])
                    eng.copy(vm[0:64, 1 - par, 0, :, 0:HD], src[64:P, 1]).then_inc(s_v, 1)

                def k_hi(G, par, at=BANK_A):
                    hi_of(kT[:, par, 0, :, 1:BPG + 1, :].rearrange("p k b c -> p k (b c)"), at, s_kp, s_kh, G)

                def exp_of(b, n, first):
                    eng.wait_ge(s_M, b + 1)
                    if not (first and n < 2):
                        eng.wait_ge(s_pv, b - 1)
                    eng.activation(probs[:, n % 2, :], S[n % 2].rearrange("p a c -> p (a c)"), ACT.Exp,
                                   scale=HD ** -0.5).then_inc(s_P, 1)

                def oT_hi(G):
                    eng.wait_ge(s_oTp, G + 1)
                    eng.copy(oT[:, 0, :, :, :].rearrange("p c b q -> p b c q"),
                             ps[:, BANK_B, :].rearrange("p (b c q) -> p b c q", b=BPG, c=2)).then_inc(s_oTh, 1)

                def zT_hi(G, stored):
                    if stored:
                        eng.wait_ge(s_zst, 16 * G)
                    hi_of(zT[:, 0, :, :], BANK_B, s_zTp, s_zTh, G)

                def step(g, half, par, old, ahead):
                    for n in range(BPG):
                        if old == 0 and n == 0:
                            eng.wait_ge(s_wAl, 2)
                        if n == BPG - 1 and ahead == 0:
                            eng.wait_ge(s_wf, 16 * (1 + EW))
                            eng.wait_ge(s_S, BPG * NG)
                            eng.copy(wF[0][:, E:E + NS, :], wfraw[:, 0:NS, :]).then_inc(s_wSh, 1)
                        exp_of(BPG * g + n, n, old == 0)
                        if n == 0 and ahead:
                            hi_of(qT[:, 0, :, :], BANK_A, s_qp, s_qh, g + 1)
                        if n == 0 and old:
                            oT_hi(g - 1)
                        if n == 1 and ahead:
                            eng.wait_ge(s_kl, g + 1)
                            eng.copy(kT[:, 1 - par, :, :, 0, :].rearrange("p a k c -> p (a k) c"),
                                     f(kT[:, par, :, :, BPG, :]).rearrange("p a k c -> p (a k) c")).then_inc(s_halo, 1)
                            k_hi(g + 1, 1 - par)
                        if n == 2 and ahead:
                            v_copy(g + 1, 1 - par)
                        if n == 3 and ahead == 2:
                            hi_of(yT[:, 0, :, :], BANK_A, s_yTp, s_yTh, g + 2)
                        if n == 3 and old:
                            zT_hi(g - 1, old >= 2)

                def prologue():
                    for h in range(2):
                        eng.wait_ge((s_w, s_w2)[h], 16)
                        eng.copy(wA[:, 0, 2 * h:2 * h + 2, :, :].rearrange("p w k c -> p (w k c)"),
                                 wraw[:, h * 1024:(h + 1) * 1024]).then_inc(s_wA, 1)
                        if h == 0:
                            hi_of(yT[:, 0, :, :], BANK_A, s_yTp, s_yTh, 0)
                    hi_of(qT[:, 0, :, :], BANK_A, s_qp, s_qh, 0)
                    k_hi(0, 0, BANK_B)
                    v_copy(0, 0)
                    hi_of(yT[:, 0, :, :], BANK_A, s_yTp, s_yTh, 1)

                def silu_of(i):
                    eng.wait_ge(s_gu, i + 1)
                    after(eng, s_hf, i - 1)
                    eng.activation(sg[:, i % NS, :], ps[:, i % NS, 0:GT], ACT.Silu).then_inc(s_sg, 1)

                def hidden_hi_of(i):
                    eng.wait_ge(s_hf, i + 1)
                    after(eng, s_yd, i - 1)
                    eng.copy(hh[i % NS][:, 0, :], hf[:, i % NS, :]).then_inc(s_hh, 1)
                    g = i // NS
                    if i % NS == NS - 1:
                        later_groups = [n for n in range(g + 1, NG) if zt_order[n] == zt_order[g]][:1]
                        for n in later_groups:
                            eng.dma_start(f(zt_of[n][0]), zT_dram[n].rearrange("p (a k c) -> p a k c", a=2, k=KT)
                                          ).then_inc(zt_of[n][1], 16)

                def expert_hi(e):
                    if e == EW:
                        eng.wait_ge(s_wf2, 16 * (E - EW))
                    eng.copy(wF[0][:, e, :], raw_of[e]).then_inc(s_wFh, 1)

                def epilogue():
                    silu_of(0)
                    expert_hi(0)
                    oT_hi(NG - 1)
                    hidden_hi_of(0)
                    expert_hi(1)
                    silu_of(1)
                    hidden_hi_of(1)
                    expert_hi(2)
                    silu_of(2)
                    expert_hi(3)
                    zT_hi(NG - 1, True)
                    hidden_hi_of(2)
                    expert_hi(4)
                sweep(eng, step, prologue, epilogue)

                def rows_hi(t, q, m):
                    eng.wait_ge(s_T, t + 1)
                    after(eng, s_g1, t - 1)
                    eng.copy(z1[:, m % 2, 0, :], ps[:, 4 + m % 2, 0:D]).then_inc(s_zh, 1)

                for i in range(3, NS * GA):
                    silu_of(i)
                    if i == NS * GA - 1:
                        eng.wait_ge(s_wFl, E)
                        rows_hi(0, 0, 0)
                        rows_hi(1, 0, 1)
                    hidden_hi_of(i)
                    if i < E - 2:
                        expert_hi(i + 2)
                    if i == 4:
                        eng.wait_ge(s_rk, 10 * NG)
                        eng.activation(esc, logits[:, :, :], ACT.Sigmoid).then_inc(s_esc, 1)
                for n in range(2, 5):
                    g = GA + n
                    eng.dma_start(f(zt_of[g][0]), zT_dram[g].rearrange("p (a k c) -> p a k c", a=2, k=KT)
                                  ).then_inc(zt_of[g][1], 16)

                def silu(t, q, m):
                    eng.wait_ge(s_g1, t + 1)
                    after(eng, s_h1, t - 1)
                    eng.activation(h1[:, m % 2, 0, :], ps[:, m % 2, 0:P], ACT.Silu).then_inc(s_s1, 1)

                def hidden_hi(t, q, m):
                    eng.wait_ge(s_hT, t + 1)
                    after(eng, s_d1, t - 1)
                    eng.copy(hT[:, m % 2, 0, :], ps[:, 6 + m % 2, 0:P]).then_inc(s_hTh, 1)

                def scaled(t, q, m):
                    eng.wait_ge(s_d1, t + 1)
                    after(eng, s_ysc[m], 16 * q)
                    w = tile_w[:, t:t + 1] if isinstance(t, int) else tile_w[:, bass.ds(t, 1)]
                    eng.activation(yo[:, m, :], ps[:, 2 + m % 2, 0:D], ACT.Copy, scale=w).then_inc(s_y1, 1)

                def tile(q, m, first, last):
                    if not (last and m >= 6):
                        rows_hi(*later(q, m, 2))
                    if not (last and m == 7):
                        silu(*later(q, m, 1))
                    hidden_hi(*later(q, m, 0))
                    if not (first and m == 0):
                        scaled(*later(q, m, -1))
                silu(0, 0, 0)
                eng.wait_ge(s_tw, 1)
                sweep_tiles(eng, tile)
                scaled(NTS - 1, NTS // 4 - 1, 3)

                for i in range(NS * GA, NS * NG):
                    silu_of(i)
                    hidden_hi_of(i)

            @block.vector
            def _(eng):
                def lo_of(dst, hi, src_bank, s_in, s_out, G):
                    eng.wait_ge(s_in, G + 1)
                    eng.tensor_tensor(dst, ps[:, src_bank, :].rearrange("p (a c) -> p a c", a=2), f(hi),
                                      ALU.subtract).then_inc(s_out, 1)

                def k_lo(G, par, at=BANK_A):
                    lo_of(kT[:, par, 1, :, 1:BPG + 1, :].rearrange("p k b c -> p k (b c)"),
                          kT[:, par, 0, :, 1:BPG + 1, :].rearrange("p k b c -> p k (b c)"), at, s_kh, s_kl, G)

                def oT_lo(G):
                    eng.wait_ge(s_oTh, G + 1)
                    eng.tensor_tensor(oT[:, 1, :, :, :].rearrange("p c b q -> p b c q"),
                                      ps[:, BANK_B, :].rearrange("p (b c q) -> p b c q", b=BPG, c=2),
                                      f(oT[:, 0, :, :, :]).rearrange("p c b q -> p b c q"),
                                      ALU.subtract).then_inc(s_oTl, 1)

                def statistics(which, G):
                    for t in range(TPG):
                        eng.bn_stats(stats[:, which, t, :], xs[:, bass.ds(TPG * G + t, 1), :].rearrange("p o d -> p (o d)")
                                     ).then_inc(s_bn[which], 1)
                    for t in range(TPG):
                        wait_apart(eng, s_bn[which], TPG * G + t + 1)
                        eng.bn_aggr(mv[:, which, t, :], stats[:, which, t, :]).then_inc(s_st[which], 1)

                def normalise(which, G, par=0, sent=False):
                    if which == 1 and sent:
                        eng.wait_ge(s_sc, 64 * (G - 1))
                    eng.wait_ge(s_rs[which], G + 1)
                    for t in range(TPG):
                        eng.tensor_scalar((y, z[:, par])[which][:, t, 0:D],
                                          xs[:, bass.ds(TPG * G + t, 1), :].rearrange("p o d -> p (o d)"),
                                          mv[:, which, t, 0:1], rstd[:, which, t:t + 1], ALU.subtract, ALU.mult
                                          ).then_inc(s_yz[which], 1)
                    if which == 1:
                        eng.tensor_copy(z[:, par, :, D], cst[:, bass.ds(TPG * G, TPG)]).then_inc(s_tok, 1)

                def maxima(b, n):
                    eng.wait_ge(s_S, b + 1)
                    eng.tensor_reduce(rmax[:, n % 2, :], S[n % 2].rearrange("p a (c q) -> p (a c) q", q=32), AX.X,
                                      ALU.max, apply_transpose=True).then_inc(s_R, 1)

                def neg_max(b, n):
                    eng.wait_ge(s_RT, b + 1)
                    eng.tensor_reduce(negm[:, n % 2, :], ps[0:32, RT, 0:P].rearrange("p (g q) -> p q g", g=4), AX.X,
                                      ALU.max, negate=True).then_inc(s_nm, 1)
                    eng.wait_ge(s_nm, b + 1)
                    eng.tensor_copy(negs[0:32, n % 2, :], negm[:, n % 2, :]).then_inc(s_nh, 1)
                    eng.wait_ge(s_nh, b + 1)
                    eng.tensor_tensor(negs[32:64, n % 2, :], negm[:, n % 2, :], f(negs[0:32, n % 2, :]),
                                      ALU.subtract).then_inc(s_nl, 1)

                def o_of(b, par, n):
                    eng.wait_ge(s_pv, b + 1)
                    for c in range(2):
                        sl = slice(64 * c, 64 * c + 64)
                        eng.reciprocal(rden[sl, :], pv[sl, :, VC * c + HD]).then_inc(s_rd, 1)
                    for c in range(2):
                        sl = slice(64 * c, 64 * c + 64)
                        eng.wait_ge(s_rd, 2 * b + c + 1)
                        eng.tensor_tensor(o[sl, par, n, :].rearrange("p (a d) -> p a d", d=HD),
                                          pv[sl, :, VC * c:VC * c + HD],
                                          rden[sl, :].unsqueeze(2).to_broadcast([64, HPT, HD]),
                                          ALU.mult).then_inc(s_o, 1)

                def residual(G):
                    eng.wait_ge(s_wo, G + 1)
                    for t in range(TPG):
                        xt = xs[:, bass.ds(TPG * G + t, 1), :].rearrange("p o d -> p (o d)")
                        eng.tensor_tensor(xt, xt, ps[:, BANK_B, t * D:(t + 1) * D], ALU.add).then_inc(s_x2, 1)
                    wait_apart(eng, s_x2, TPG * (G + 1))

                def logits_add(G):
                    eng.wait_ge(s_lgp, G + 1)
                    eng.tensor_reduce(logits[:, bass.ds(TPG * G, TPG), :],
                                      ps[:, BANK_B, 0:32].rearrange("p (t a e) -> p t e a", t=2, a=2), AX.X,
                                      ALU.add).then_inc(s_lg, 1)

                def link(ins, value):
                    ins.then_inc(s_rk, 1)
                    eng.wait_ge(s_rk, value)

                def comparisons(G):
                    lg = logits[:, bass.ds(TPG * G, TPG), :]
                    other = lg.unsqueeze(2).to_broadcast([P, TPG, E, E])
                    own = lg.unsqueeze(3).to_broadcast([P, TPG, E, E])
                    lower = const("lower").rearrange("p (e f) -> p e f", e=E).unsqueeze(1).to_broadcast([P, TPG, E, E])
                    eng.wait_ge(s_lg, G + 1)
                    link(eng.tensor_tensor(lg, lg, biasb[:, :].unsqueeze(1).to_broadcast([P, TPG, E]), ALU.add), 10 * G + 1)
                    eng.tensor_tensor(cmp_gt[:, :, :, :], other, own, ALU.is_gt).then_inc(s_rk, 1)
                    link(eng.tensor_tensor(cmp_eq[:, :, :, :], other, own, ALU.is_equal), 10 * G + 3)
                    link(eng.tensor_tensor(cmp_eq[:, :, :, :], cmp_eq[:, :, :, :], lower, ALU.mult), 10 * G + 4)

                def ranks(G):
                    link(eng.tensor_tensor(cmp_gt[:, :, :, :], cmp_gt[:, :, :, :], cmp_eq[:, :, :, :], ALU.add), 10 * G + 5)
                    link(eng.tensor_reduce(rank[:, :, :], cmp_gt[:, :, :, :], AX.X, ALU.add), 10 * G + 6)
                    eng.tensor_scalar(sel[:, bass.ds(TPG * G, TPG), :], rank[:, :, :], 1.0 * K, None,
                                      ALU.is_lt).then_inc(s_rk, 1)
                    eng.tensor_tensor(chosen[:, :, :, :], rank[:, :, :].unsqueeze(1).to_broadcast([P, K, TPG, E]),
                                      const("choice").unsqueeze(2).unsqueeze(3).to_broadcast([P, K, TPG, E]),
                                      ALU.is_equal).then_inc(s_rk, 1)

                def first_expert(G, par):
                    eng.wait_ge(s_rk, 10 * G + 8)
                    link(eng.tensor_tensor(cmp_gt[:, :, 0, :], chosen[:, 0, :, :],
                                           const("expert").unsqueeze(1).to_broadcast([P, TPG, E]), ALU.mult), 10 * G + 9)
                    link(eng.tensor_reduce(z[:, par, :, D + 1], cmp_gt[:, :, 0, :], AX.X, ALU.add), 10 * G + 10)

                def routing(G, par):
                    comparisons(G)
                    ranks(G)
                    first_expert(G, par)

                def places(G, par):
                    eng.wait_ge(s_cum, G + 1)
                    eng.tensor_tensor(slots[:, :, :], ps[:, RT, 256:256 + TPG * E].rearrange("p (t e) -> p t e", e=E),
                                      const("region").unsqueeze(1).to_broadcast([P, TPG, E]), ALU.add).then_inc(s_sl, 1)
                    eng.tensor_tensor(seen[:, :], seen[:, :], sel[:, bass.ds(TPG * G, 1), :].rearrange("p o e -> p (o e)"),
                                      ALU.add).then_inc(s_sl, 1)
                    eng.wait_ge(s_sl, 5 * G + 2)
                    eng.tensor_tensor(slot_of[:, :, :, :], slots[:, :, :].unsqueeze(1).to_broadcast([P, K, TPG, E]),
                                      chosen[:, :, :, :], ALU.mult).then_inc(s_sl, 1)
                    eng.tensor_tensor(seen[:, :], seen[:, :], sel[:, bass.ds(TPG * G + 1, 1), :].rearrange("p o e -> p (o e)"),
                                      ALU.add).then_inc(s_sl, 1)
                    eng.wait_ge(s_sl, 5 * G + 4)
                    eng.tensor_reduce(slot_f[:, :, :], slot_of[:, :, :, :], AX.X, ALU.add).then_inc(s_sl, 1)
                    eng.wait_ge(s_sl, 5 * G + 5)
                    eng.tensor_copy(slot[:, par, :, :], slot_f[:, :, :]).then_inc(s_ix, 1)

                def step(g, half, par, old, ahead):
                    for n in range(BPG):
                        b = BPG * g + n
                        n2 = (n + 1) % BPG
                        if n == 2 and old == 3:
                            places(g - 3, 1 - par)
                        if ahead or n < BPG - 1:
                            maxima(b + 1, n2)
                        if n == 0 and old == 3:
                            comparisons(g - 3)
                        if n == 1 and old == 3:
                            ranks(g - 3)
                        if n == 3 and old:
                            normalise(1, g - 1, 1 - par, old == 3)
                        if ahead or n < BPG - 1:
                            neg_max(b + 1, n2)
                        if n == 1 and old == 3:
                            first_expert(g - 3, 1 - par)
                        if n == BPG - 1 and ahead == 0:
                            routing(NG - 3, 1)
                        if old or n:
                            o_of(b - 1, par if n else 1 - par, (n - 1) % BPG)
                        if n == BPG - 1 and ahead == 0:
                            eng.wait_ge(s_wSh, 1)
                            eng.tensor_tensor(wF[1][:, E:E + NS, :], wfraw[:, 0:NS, :], f(wF[0][:, E:E + NS, :]),
                                              ALU.subtract).then_inc(s_wSl, 1)
                        if n == 2 and old:
                            residual(g - 1)
                        if n == 0:
                            if ahead:
                                lo_of(qT[:, 1, :, :], qT[:, 0, :, :], BANK_A, s_qh, s_ql, g + 1)
                            if ahead == 2:
                                for c in (1,) if old == 0 else range(2, XC) if old == 2 else ():
                                    eng.wait_ge(s_x[c], 16)
                                statistics(0, g + 2)
                            if old:
                                oT_lo(g - 1)
                        if n == 1:
                            if ahead:
                                k_lo(g + 1, 1 - par)
                            if ahead == 2:
                                normalise(0, g + 2)
                        if n == 2:
                            if old:
                                statistics(1, g - 1)
                            if old >= 2:
                                logits_add(g - 2)
                        if n == 3:
                            if ahead == 2:
                                lo_of(yT[:, 1, :, :], yT[:, 0, :, :], BANK_A, s_yTh, s_yTl, g + 2)
                            if old:
                                lo_of(zT[:, 1, :, :], zT[:, 0, :, :], BANK_B, s_zTh, s_zTl, g - 1)

                def prologue():
                    eng.memset(vt[:, :, :, :, :], 1.0).then_inc(s_v1, 1)
                    eng.memset(vm[:, :, :, :, :], 1.0).then_inc(s_v1, 1)
                    eng.memset(f(kT[:, 0, :, :, 0, :]), 0.0).then_inc(s_v1, 1)
                    eng.wait_ge(s_x[0], 16)
                    statistics(0, 0)
                    normalise(0, 0)

                    def weights_lo(h):
                        eng.wait_ge(s_wA, h + 1)
                        eng.tensor_tensor(wA[:, 1, 2 * h:2 * h + 2, :, :].rearrange("p w k c -> p (w k c)"),
                                          wraw[:, h * 1024:(h + 1) * 1024],
                                          f(wA[:, 0, 2 * h:2 * h + 2, :, :]).rearrange("p w k c -> p (w k c)"),
                                          ALU.subtract).then_inc(s_wAl, 1)
                    weights_lo(0)
                    lo_of(yT[:, 1, :, :], yT[:, 0, :, :], BANK_A, s_yTh, s_yTl, 0)
                    statistics(0, 1)
                    weights_lo(1)
                    lo_of(qT[:, 1, :, :], qT[:, 0, :, :], BANK_A, s_qh, s_ql, 0)
                    normalise(0, 1)
                    k_lo(0, 0, BANK_B)
                    lo_of(yT[:, 1, :, :], yT[:, 0, :, :], BANK_A, s_yTh, s_yTl, 1)
                    eng.wait_ge(s_const, 48)
                    eng.memset(f(wG[:, 1, :, 1, :]), 0.0).then_inc(s_wG, 1)
                    eng.tensor_copy(wG[:, 0, :, 0, :], graw[:, :, :]).then_inc(s_wG, 1)
                    eng.tensor_copy(wG[:, 1, :, 0, :], graw[:, :, :]).then_inc(s_wG, 1)
                    eng.wait_ge(s_wG, 3)
                    eng.tensor_tensor(wG[:, 0, :, 1, :], graw[:, :, :], f(wG[:, 0, :, 0, :]), ALU.subtract).then_inc(s_wG, 1)
                    maxima(0, 0)
                    neg_max(0, 0)

                def hidden_of(i):
                    eng.wait_ge(s_sg, i + 1)
                    after(eng, s_hl, i - 1)
                    e = i % NS
                    eng.tensor_tensor(hf[:, e, :], sg[:, e, :], ps[:, e, GT:2 * GT], ALU.mult).then_inc(s_hf, 1)

                def accumulate(i):
                    g, e = i // NS, i % NS
                    eng.wait_ge(s_yd, i + 1)
                    after(eng, s_acc, i)
                    xg = xs[:, TPG * g:TPG * (g + 1), :].rearrange("p t d -> p (t d)")
                    eng.tensor_tensor(xg, xg, ps[:, 2 + e, :], ALU.add).then_inc(s_acc, 1)

                def hidden_lo_of(i):
                    e = i % NS
                    eng.wait_ge(s_hh, i + 1)
                    eng.tensor_tensor(hh[e][:, 1, :], hf[:, e, :], f(hh[e][:, 0, :]), ALU.subtract).then_inc(s_hl, 1)

                def epilogue():
                    places(NG - 3, 1)
                    o_of(BPG * NG - 1, 1, BPG - 1)
                    hidden_of(0)
                    oT_lo(NG - 1)
                    hidden_lo_of(0)
                    hidden_of(1)
                    residual(NG - 1)
                    statistics(1, NG - 1)
                    accumulate(0)
                    logits_add(NG - 2)
                    hidden_lo_of(1)
                    hidden_of(2)
                    normalise(1, NG - 1, 1, True)
                    routing(NG - 2, 0)
                    lo_of(zT[:, 1, :, :], zT[:, 0, :, :], BANK_B, s_zTh, s_zTl, NG - 1)
                    places(NG - 2, 0)
                    accumulate(1)
                    hidden_lo_of(2)
                    hidden_of(3)
                    logits_add(NG - 1)
                    routing(NG - 1, 1)
                    accumulate(2)
                    hidden_lo_of(3)
                    hidden_of(4)
                    places(NG - 1, 1)
                sweep(eng, step, prologue, epilogue)

                count = [0]

                def link(ins):
                    count[0] += 1
                    ins.then_inc(s_rt, 1)
                    eng.wait_ge(s_rt, count[0])

                tokens, tiles, tiles_end, mean_w = (counts[:, i, :] for i in range(4))

                def over_tiles(ap):
                    return ap.unsqueeze(1).to_broadcast([P, NTS, E])

                def count_tiles():
                    eng.wait_ge(s_cnt, 1)
                    eng.wait_ge(s_pv, BPG * NG)
                    link(eng.tensor_copy(tokens, ps[:, RT, 288:288 + E]))
                    eng.tensor_tensor(fill_at[:, :], tokens, const("region"), ALU.add).then_inc(s_fo, 1)
                    link(eng.tensor_tensor(few, tokens.unsqueeze(2).to_broadcast([P, E, NT]),
                                           const("tile_rows").unsqueeze(1).to_broadcast([P, E, NT]), ALU.is_gt))
                    link(eng.tensor_reduce(tiles, few, AX.X, ALU.add))
                    link(eng.tensor_tensor(few[:, :, 0:E], tiles.unsqueeze(1).to_broadcast([P, E, E]),
                                           const("upto").rearrange("p (e f) -> p e f", e=E), ALU.mult))
                    link(eng.tensor_reduce(tiles_end, few[:, :, 0:E], AX.X, ALU.add))

                def tile_table():
                    link(eng.tensor_tensor(table[0], const("tile").unsqueeze(2).to_broadcast([P, NTS, E]),
                                           over_tiles(tiles_end), ALU.is_ge))
                    link(eng.tensor_reduce(tile_e[:, :], table[0], AX.X, ALU.add))
                    link(eng.tensor_tensor(table[0], table[0], over_tiles(tiles), ALU.mult))
                    link(eng.tensor_reduce(tile_w[:, :], table[0], AX.X, ALU.add))

                def tile_places():
                    link(eng.tensor_tensor(tile_w[:, :], const("tile"), tile_w[:, :], ALU.subtract))
                    link(eng.tensor_scalar(table[0][:, :, 0], tile_e[:, :], 1.0 * REGION, None, ALU.mult))
                    link(eng.tensor_scalar(tile_w[:, :], tile_w[:, :], 1.0 * P, None, ALU.mult))
                    link(eng.tensor_tensor(tile_w[:, :], tile_w[:, :], table[0][:, :, 0], ALU.add))
                    link(eng.memset(tile_ei[:, :], 0))
                    link(eng.tensor_scalar(tile_ei[:, 1:NTS + 1], tile_e[:, :], 1.0 * (E - 1), None, ALU.min))
                    link(eng.tensor_scalar(tile_row[:, :], tile_w[:, :], 1.0 * E * REGION, None, ALU.min))
                    eng.memset(h1[:, 0, 0, 0:1], 0.0).then_inc(s_tab, 1)

                def token_weights():
                    eng.wait_ge(s_esc, 1)
                    link(eng.tensor_tensor(esc, esc, sel[:, :, :], ALU.mult))
                    link(eng.tensor_reduce(token_sum, esc, AX.X, ALU.add))

                def weight_sums():
                    link(eng.tensor_scalar(token_sum, token_sum, 1e-8, None, ALU.add))
                    link(eng.reciprocal(token_sum, token_sum))
                    link(eng.tensor_tensor(esc, esc, token_sum.unsqueeze(2).to_broadcast([P, NT, E]), ALU.mult))
                    eng.tensor_reduce(wsum, esc.rearrange("p t e -> p e t"), AX.X, ALU.add).then_inc(s_cs, 1)

                def mean_weights():
                    eng.wait_ge(s_tot, 1)
                    link(eng.tensor_scalar(mean_w, tokens, 1.0, None, ALU.max))
                    link(eng.reciprocal(mean_w, mean_w))
                    link(eng.tensor_tensor(mean_w, mean_w, ps[:, BANK_B, 0:E], ALU.mult))

                def tile_weights():
                    link(eng.tensor_tensor(table[1], tile_e[:, :].unsqueeze(2).to_broadcast([P, NTS, E]),
                                           over_tiles(const("expert")), ALU.is_equal))
                    link(eng.tensor_tensor(table[1], table[1], over_tiles(mean_w), ALU.mult))
                    eng.tensor_reduce(tile_w[:, :], table[1], AX.X, ALU.add).then_inc(s_tw, 1)

                between = {4: count_tiles, 5: tile_table, 6: tile_places, 7: token_weights, 8: weight_sums, 9: mean_weights,
                           10: tile_weights}
                def rows_lo(t, q, m):
                    eng.wait_ge(s_zh, t + 1)
                    eng.tensor_tensor(z1[:, m % 2, 1, :], ps[:, 4 + m % 2, 0:D], f(z1[:, m % 2, 0, :]),
                                      ALU.subtract).then_inc(s_zl, 1)

                def destinations(t, q, m):
                    eng.wait_ge(s_zin[m], 16 * (q + 1))
                    ef = tile_e[:, t:t + 1] if isinstance(t, int) else tile_e[:, bass.ds(t, 1)]
                    eng.tensor_scalar(dest_f[:, m:m + 1], zin[:, m, D + 1:D + 2], ef, 1.0 * T,
                                      ALU.not_equal, ALU.mult).then_inc(s_df, 1)
                    eng.wait_ge(s_df, 2 * t + 1)
                    eng.tensor_tensor(dest_f[:, m:m + 1], dest_f[:, m:m + 1], zin[:, m, D:D + 1], ALU.add).then_inc(s_df, 1)

                for i in range(4, NS * GA):
                    if i > 4:
                        hidden_of(i)
                    if i == NS * GA - 1:
                        for t in range(2):
                            rows_lo(t, 0, t)
                            destinations(t, 0, t)
                        hidden_lo_of(i)
                    accumulate(i - 1)
                    if i < NS * GA - 1:
                        hidden_lo_of(i)
                    if i in between:
                        between[i]()

                def hidden(t, q, m):
                    eng.wait_ge(s_s1, t + 1)
                    after(eng, s_hT, t - 1)
                    eng.tensor_tensor(h1[:, m % 2, 1, :], h1[:, m % 2, 0, :], ps[:, m % 2, P:2 * P], ALU.mult).then_inc(s_h1, 1)

                def hidden_lo(t, q, m):
                    eng.wait_ge(s_hTh, t + 1)
                    eng.tensor_tensor(hT[:, m % 2, 1, :], ps[:, 6 + m % 2, 0:P], f(hT[:, m % 2, 0, :]),
                                      ALU.subtract).then_inc(s_hTl, 1)

                def destinations_int(t, q, m):
                    eng.wait_ge(s_df, 2 * t + 2)
                    after(eng, s_ysc[m], 16 * q)
                    eng.tensor_copy(dest[:, m:m + 1], dest_f[:, m:m + 1]).then_inc(s_ds, 1)

                def tile(q, m, first, last):
                    if not (last and m >= 6):
                        rows_lo(*later(q, m, 2))
                        destinations(*later(q, m, 2))
                    if not (last and m == 7):
                        hidden(*later(q, m, 1))
                    hidden_lo(*later(q, m, 0))
                    destinations_int(*later(q, m, 0))
                hidden(0, 0, 0)
                accumulate(NS * GA - 1)
                sweep_tiles(eng, tile)

                def combined(g):
                    eng.wait_ge(s_yy, g + 1)
                    eng.wait_ge(s_acc, NS * (max(g, GA - 1) + 1))
                    eng.tensor_tensor(xs[:, TPG * g:TPG * (g + 1), :], xs[:, TPG * g:TPG * (g + 1), :],
                                      ya[g % 4][:, 0, :, :], ALU.add).then_inc(s_cb, 1)

                for i in range(NS * GA, NS * NG):
                    hidden_of(i)
                    if i > NS * GA:
                        accumulate(i - 1)
                    hidden_lo_of(i)
                    if i > NS * GA + 2 and i - NS * GA - 3 < NG - 3:
                        combined(i - NS * GA - 3)
                combined(NG - 3)
                combined(NG - 2)
                accumulate(NS * NG - 1)
                combined(NG - 1)


def kernel(**inputs):
    import numpy as np
    import concourse.bacc as bacc
    from concourse import mybir as my
    from concourse.bass_utils import run_bass_kernel_spmd

    def transposed(w):
        return w.T.reshape(KT, P, w.shape[0]).transpose(1, 0, 2)

    a = {k: np.asarray(v) for k, v in inputs.items()}
    x = a["L0_attn_hidden"]
    wo = a["L0_attn_Wo"].T.reshape(HPT, 2, HD, D).transpose(0, 2, 1, 3).reshape(P, 2, D)
    wqkvo = np.stack([transposed(a["L0_attn_Wq"]), transposed(a["L0_attn_Wk"]), transposed(a["L0_attn_Wv"]), wo], 1)

    def expert(gate, up, down):
        return np.concatenate([np.stack([transposed(gate), transposed(up)], 2).reshape(P, -1), down.T], 1)

    ffn = [expert(a["L0_ffn_expert_gate_w"][e], a["L0_ffn_expert_up_w"][e], a["L0_ffn_expert_down_w"][e])
           for e in range(E)]
    for i in range(0, a["L0_ffn_shared_gate_w"].shape[0], EI):
        ffn.append(expert(a["L0_ffn_shared_gate_w"][i:i + EI], a["L0_ffn_shared_up_w"][i:i + EI],
                          a["L0_ffn_shared_down_w"][:, i:i + EI]))
    T = x.shape[0] * x.shape[1]
    e, p = np.arange(E), np.arange(P)
    values = {
        "token": p[:, None] + P * np.arange(T // P),
        "before": p[:, None] < p,
        "region": e * (T + P),
        "expert": e,
        "lower": (e[:, None] > e).reshape(-1),
        "upto": (e[:, None] >= e).reshape(-1),
        "tile_rows": P * np.arange(T // P),
        "tile": np.arange(expert_tiles(T)),
        "choice": np.arange(K),
    }
    at, n = constants(T)
    consts = np.zeros((P, n), np.float32)
    for name, (c, w) in at.items():
        consts[:, c:c + w] = values[name]
    arrays = {
        "x": x.reshape(-1, D),
        "wqkvo": wqkvo.reshape(P, -1),
        "wgate": transposed(a["L0_ffn_gate_w"]),
        "bias": a["L0_ffn_lb_bias"],
        "wffn": np.stack(ffn, 1),
        "identity": np.eye(P, dtype=np.float32),
        "consts": consts,
    }
    arrays = {k: np.ascontiguousarray(v) for k, v in arrays.items()}
    nc = bacc.Bacc("TRN2", target_bir_lowering=False, num_devices=1)
    args = [nc.dram_tensor(k, v.shape, my.dt.from_np(v.dtype), kind="ExternalInput").ap() for k, v in arrays.items()]
    args.append(nc.dram_tensor("out", arrays["x"].shape, my.dt.float32, kind="ExternalOutput").ap())
    layer(nc, *args)
    r = run_bass_kernel_spmd(nc, [arrays], core_ids=[0])
    return r.results[0]["out"].reshape(x.shape)
```
